# Optimizing a Trainium2 kernel written in Bass

```python
import numpy as np
import jax
import jax.numpy as jnp

def _softmax(x, axis=-1):
    return jax.nn.softmax(x, axis=axis)

def _gelu(x):
    return jax.nn.gelu(x, approximate=True)

def _silu(x):
    return jax.nn.silu(x)

def _sigmoid(x):
    return jax.nn.sigmoid(x)

def _layernorm(x, axis=-1, eps=1e-05):
    m = jnp.mean(x, axis=axis, keepdims=True)
    v = jnp.var(x, axis=axis, keepdims=True)
    return (x - m) / jnp.sqrt(v + eps)

def _scatter_add(tgt, idx, src, axis=0):
    return tgt.at[idx].add(src)

def _segment_sum(src, seg, n):
    return jax.ops.segment_sum(src, seg, n)
kernel_name = 'mk_conv_attn_hybrid_d2_conv_nhwc384_r4_7c83ae'

def setup_inputs(seed: int=0):
    np.random.seed(seed)
    _w = jnp.asarray

    def _rec_inputs():
        import jax
        import jax.numpy as jnp
        _gk = jax.random.key(seed)
        x = -0.0002221 + 1 * jax.random.normal(jax.random.fold_in(_gk, 1), (16, 16, 16, 96), jnp.float32)
        return x
    x = _rec_inputs()

    def _L0_conv_setup():
        import jax, jax.numpy as jnp
        import numpy as np
        B, H, W, C, E, TOP_K = (16, 16, 16, 96, 5, 2)
        key = jax.random.key(seed)
        k1, k2, k3 = jax.random.split(key, 3)
        x = jax.random.normal(k1, (B, H, W, C), dtype=jnp.float32)
        Wg = jax.random.normal(k2, (C, E), dtype=jnp.float32) * 0.02
        We = jax.random.normal(k3, (E, C, C), dtype=jnp.float32) * 0.02
        be = jnp.zeros((E, C), dtype=jnp.float32)
        return {'x': x, 'Wg': Wg, 'We': We, 'be': be}
    _L0_conv_all = _L0_conv_setup()
    _L0_conv_in = {k: v for k, v in _L0_conv_all.items() if k in ('Wg', 'We', 'be')}
    del _L0_conv_all

    def _L1_attn_setup():
        import jax, jax.numpy as jnp
        import numpy as np
        N_EMB = 96
        BLOCK_SIZE = 64
        key = jax.random.key(seed)
        ks = jax.random.split(key, 6)
        B, T, H, D = (64, 64, 6, 16)
        x = jax.random.normal(ks[0], (B, T, N_EMB), dtype=jnp.float32)
        wk = jax.random.normal(ks[1], (H, N_EMB, D), dtype=jnp.float32) * N_EMB ** (-0.5)
        wq = jax.random.normal(ks[2], (H, N_EMB, D), dtype=jnp.float32) * N_EMB ** (-0.5)
        wv = jax.random.normal(ks[3], (H, N_EMB, D), dtype=jnp.float32) * N_EMB ** (-0.5)
        wproj = jax.random.normal(ks[4], (N_EMB, N_EMB), dtype=jnp.float32) * N_EMB ** (-0.5)
        bproj = jnp.zeros((N_EMB,), dtype=jnp.float32)
        return {'x': x, 'wk': wk, 'wq': wq, 'wv': wv, 'wproj': wproj, 'bproj': bproj}
    _L1_attn_all = _L1_attn_setup()
    _L1_attn_in = {k: v for k, v in _L1_attn_all.items() if k in ('wk', 'wq', 'wv', 'wproj', 'bproj')}
    del _L1_attn_all

    def _L1_ffn_setup():
        import jax, jax.numpy as jnp
        import numpy as np
        NUM_EXPERTS = 4
        TOP_K = 2
        DIM = 96
        HID = 4 * DIM
        key = jax.random.key(seed)
        ks = jax.random.split(key, 5)
        B, S = (16, 512)
        scale_in = 1.0 / np.sqrt(DIM)
        scale_hid = 1.0 / np.sqrt(HID)
        return {'x': jax.random.normal(ks[0], (B, S, DIM), dtype=jnp.float32), 'gate_w': jax.random.normal(ks[1], (DIM, NUM_EXPERTS), dtype=jnp.float32) * scale_in, 'gate_b': jnp.zeros((NUM_EXPERTS,), dtype=jnp.float32), 'w1': jax.random.normal(ks[2], (NUM_EXPERTS, DIM, HID), dtype=jnp.float32) * scale_in, 'b1': jnp.zeros((NUM_EXPERTS, HID), dtype=jnp.float32), 'w2': jax.random.normal(ks[3], (NUM_EXPERTS, HID, DIM), dtype=jnp.float32) * scale_hid, 'b2': jnp.zeros((NUM_EXPERTS, DIM), dtype=jnp.float32)}
    _L1_ffn_all = _L1_ffn_setup()
    _L1_ffn_in = {k: v for k, v in _L1_ffn_all.items() if k in ('gate_w', 'gate_b', 'w1', 'b1', 'w2', 'b2')}
    del _L1_ffn_all
    return {'x': x, 'L0_conv_Wg': _L0_conv_in['Wg'], 'L0_conv_We': _L0_conv_in['We'], 'L0_conv_be': _L0_conv_in['be'], 'L1_attn_wk': _L1_attn_in['wk'], 'L1_attn_wq': _L1_attn_in['wq'], 'L1_attn_wv': _L1_attn_in['wv'], 'L1_attn_wproj': _L1_attn_in['wproj'], 'L1_attn_bproj': _L1_attn_in['bproj'], 'L1_ffn_gate_w': _L1_ffn_in['gate_w'], 'L1_ffn_gate_b': _L1_ffn_in['gate_b'], 'L1_ffn_w1': _L1_ffn_in['w1'], 'L1_ffn_b1': _L1_ffn_in['b1'], 'L1_ffn_w2': _L1_ffn_in['w2'], 'L1_ffn_b2': _L1_ffn_in['b2']}

def reference(x, L0_conv_Wg, L0_conv_We, L0_conv_be, L1_attn_wk, L1_attn_wq, L1_attn_wv, L1_attn_wproj, L1_attn_bproj, L1_ffn_gate_w, L1_ffn_gate_b, L1_ffn_w1, L1_ffn_b1, L1_ffn_w2, L1_ffn_b2):
    import jax
    import jax.numpy as jnp

    def _L0_conv_ref(x, Wg, We, be):
        import jax, jax.numpy as jnp
        import numpy as np
        B, H, W, C, E, TOP_K = (16, 16, 16, 96, 5, 2)
        Bx, Hx, Wx, Cx = x.shape
        Ex = Wg.shape[1]
        t = x.reshape(-1, Cx)
        N = t.shape[0]
        logits = t @ Wg
        top_vals, top_idx = jax.lax.top_k(logits, TOP_K)
        gates = jax.nn.softmax(top_vals, axis=-1)
        combine = jnp.zeros((N, Ex), dtype=t.dtype)
        combine = combine.at[jnp.arange(N)[:, None], top_idx].set(gates)
        expert_out = jnp.einsum('nc,ecd->ned', t, We) + be[None]
        y = jnp.einsum('ne,ned->nd', combine, expert_out)
        y = jax.nn.leaky_relu(y, negative_slope=0.01)
        return y.reshape(Bx, Hx, Wx, Cx)

    def _L1_attn_ref(x, wk, wq, wv, wproj, bproj):
        import jax, jax.numpy as jnp
        import numpy as np
        N_EMB = 96
        BLOCK_SIZE = 64
        B, T, C = x.shape
        k = jnp.einsum('btc,hcd->bhtd', x, wk)
        q = jnp.einsum('btc,hcd->bhtd', x, wq)
        v = jnp.einsum('btc,hcd->bhtd', x, wv)
        wei = jnp.einsum('bhtd,bhsd->bhts', k, q) / C ** 0.5
        causal = jnp.tril(jnp.ones((T, T), dtype=bool))
        wei = jnp.where(causal, wei, -jnp.inf)
        wei = jax.nn.softmax(wei, axis=-1)
        out = jnp.einsum('bhts,bhsd->bhtd', wei, v)
        out = out.transpose(0, 2, 1, 3).reshape(B, T, C)
        out = out @ wproj + bproj
        return out

    def _L1_ffn_ref(x, gate_w, gate_b, w1, b1, w2, b2):
        import jax, jax.numpy as jnp
        import numpy as np
        NUM_EXPERTS = 4
        TOP_K = 2
        DIM = 96
        HID = 4 * DIM
        scores = jnp.einsum('bsd,de->bse', x, gate_w) + gate_b
        probs = jax.nn.softmax(scores, axis=-1)
        topk_vals, topk_idx = jax.lax.top_k(probs, TOP_K)
        mask = jnp.sum(jax.nn.one_hot(topk_idx, NUM_EXPERTS, dtype=probs.dtype), axis=-2)
        masked = probs * mask
        masked = masked / (jnp.sum(masked, axis=-1, keepdims=True) + 1e-09)
        h = jax.nn.gelu(jnp.einsum('bsd,edh->ebsh', x, w1) + b1[:, None, None, :], approximate=False)
        y = jnp.einsum('ebsh,ehd->ebsd', h, w2) + b2[:, None, None, :]
        out = jnp.einsum('bse,ebsd->bsd', masked, y)
        return out

    def _gn(v, G=32, eps=1e-05):
        B_, H_, W_, C_ = v.shape
        g = v.reshape(B_, H_, W_, G, C_ // G)
        m = jnp.mean(g, axis=(1, 2, 4), keepdims=True)
        s = jnp.var(g, axis=(1, 2, 4), keepdims=True)
        return ((g - m) / jnp.sqrt(s + eps)).reshape(v.shape)

    def _ln_c(v, eps=1e-06):
        m = jnp.mean(v, axis=-1, keepdims=True)
        s = jnp.var(v, axis=-1, keepdims=True)
        return (v - m) / jnp.sqrt(s + eps)

    def _ln_t(v, eps=1e-05):
        m = jnp.mean(v, axis=-1, keepdims=True)
        s = jnp.var(v, axis=-1, keepdims=True)
        return (v - m) / jnp.sqrt(s + eps)

    def _to_tokens(v):
        B_, H_, W_, C_ = v.shape
        return v.reshape(B_, H_ * W_, C_)

    def _from_tokens(t, like):
        return t.reshape(like.shape)
    x = x + _L0_conv_ref(_gn(x), L0_conv_Wg, L0_conv_We, L0_conv_be)
    t = _to_tokens(x)
    t = t + _L1_attn_ref(_ln_t(t), L1_attn_wk, L1_attn_wq, L1_attn_wv, L1_attn_wproj, L1_attn_bproj)
    t = t + _L1_ffn_ref(_ln_t(t), L1_ffn_gate_w, L1_ffn_gate_b, L1_ffn_w1, L1_ffn_b1, L1_ffn_w2, L1_ffn_b2)
    x = _from_tokens(t, x)
    return x

_drawn_inputs = setup_inputs


def setup_inputs(seed=0):
    import zlib

    import numpy as np

    out = dict(_drawn_inputs(seed))
    spreads = {'L0_conv_be': (0.0, 0.1),
     'L1_attn_bproj': (0.0, 0.1),
     'L1_ffn_gate_b': (0.0, 0.1),
     'L1_ffn_b1': (0.0, 0.1),
     'L1_ffn_b2': (0.0, 0.1)}
    factors = {}
    for name, (base, spread) in spreads.items():
        noise = np.random.default_rng([zlib.crc32(name.encode()), seed]).standard_normal(out[name].shape)
        drawn = base * np.exp(spread * noise) if base else spread * noise
        out[name] = jnp.asarray(drawn.astype(out[name].dtype))
    for name, factor in factors.items():
        out[name] = (out[name] * factor).astype(out[name].dtype)
    return out
```

```python
from contextlib import ExitStack

import concourse.bass as bass
from concourse import mybir

ALU = mybir.AluOpType
ACT = mybir.ActivationFunctionType
AX_X = mybir.AxisListType.X
F32 = mybir.dt.float32
F32R = mybir.dt.float32r
BF16 = mybir.dt.bfloat16

P = 128
IMAGES, TOKENS, C = 16, 256, 96
GROUPS = 32
GC = C // GROUPS
E0 = 5
E1 = 4
HEADS, D = 6, 16
HID = 384
TILES = 4
PT = TILES * P
PAIRS = IMAGES * TOKENS // PT
CHUNKS = HID // P
BLOCKS = E1 * CHUNKS
HG = 3
HS = 32
CONV_N = E0 * C + E0 + 1
SCALE = float(C) ** -0.5
MASKED = -1.0e30
K_PARTS = (0, 0, 1, 0, 2, 1)
Q_PARTS = (0, 1, 0, 2, 0, 1)
STACK = len(K_PARTS) * D
SHIFT = 3
X_LOADS = 4

SCHEDULE = (
    [("ffn1", 0), ("ffn1", 1), ("conv",), ("gates",), ("ffn1", 2), ("ffn1", 3), ("ffn1", 4), ("mix",),
     ("ffn1", 5), ("ffn1", 6), ("ffn1", 7), ("norm1_t",), ("ffn1", 8), ("qk",), ("v",), ("ffn1", 9),
     ("ffn1", 10), ("ffn1", 11), ("xn",), ("ffn2", 0)]
    + [("score", 0, k) for k in range(5)] + [("ffn2", 1)]
    + [("score", 1, k) for k in range(5)]
    + [("shift",), ("ffn2", 2)]
    + [("prob", 0, k) for k in range(5)] + [("prob", 1, k) for k in range(2)] + [("pv", 0)]
    + [("prob", 1, k) for k in range(2, 5)] + [("out_t", 0), ("pv", 1), ("out_t", 1), ("ffn2", 3)]
    + [("heads_t",), ("proj",), ("norm2_t",), ("gate2",)]
)

RING = 4
ROLLED = True
UNFUSED = 2
DRAINS = {"conv": "V", "norm1_t": "SV", "q": "SV", "k": "SV", "v": "S", "score": "V", "shift": "S",
          "prob": "S", "pv": "S", "out_t": "V", "heads_t": "S", "proj": "V", "norm2_t": "SV", "gate2": "V"}


def list_fills():
    fills = []
    for step in SCHEDULE:
        if step[0] == "conv":
            fills += [("conv", t) for t in range(TILES)]
        elif step[0] == "qk":
            fills += [("q",), ("k",)]
        elif step[0] in DRAINS:
            fills.append(step)
    return fills


FILLS = list_fills()
DVE_STEPS = 57
POOL_STEPS = 4


def at(i, per, n):
    return i * per + n


def build(nc, x, conv_gate, conv_w, conv_b, wk, wq, wv, wproj, bproj, gate_w, gate_b, w1, b1, w2, b2, out):
    x_t = x.rearrange("b h w c -> (b h w) c").rearrange("(t p) c -> p t c", p=P)
    out_t = out.rearrange("b h w c -> (b h w) c").rearrange("(t p) c -> p t c", p=P)

    with ExitStack() as ctx:
        def sb(name, shape, dt=F32):
            return ctx.enter_context(nc.sbuf_tensor(name, shape, dt))

        def sem(name):
            return ctx.enter_context(nc.semaphore(name))

        PS = ctx.enter_context(nc.psum_tensor("PS", [P, 8, 512], F32))

        ones = sb("ones", [P, P])
        ident = sb("ident", [P, P])
        ident_b = sb("ident_b", [P, P], BF16)
        zeros_b = sb("zeros_b", [P, P], BF16)
        causal_b = sb("causal_b", [P, P], BF16)
        group_avg = sb("group_avg", [C, C])
        ones_b = sb("ones_b", [C, P], BF16)
        before0 = sb("before0", [P, E0, E0])
        before1 = sb("before1", [P, E1, E1])
        eps_t = sb("eps_t", [P, 32])
        power_t = sb("power_t", [P, 32])
        conv_f = sb("conv_f", [C + 1, CONV_N])
        conv_hi = sb("conv_hi", [C + 1, CONV_N], F32R)
        conv_lo = sb("conv_lo", [C + 1, CONV_N], F32R)
        qk_f = sb("qk_f", [C, 2, HEADS, D])
        qk_hi = sb("qk_hi", [C, 2, C], F32R)
        qk_lo = sb("qk_lo", [C, 2, C], F32R)
        wv_f = sb("wv_f", [C, HEADS, D])
        wproj_f = sb("wproj_f", [C + 1, C])
        gate_f = sb("gate_f", [C + 1, C])
        w1_f = sb("w1_f", [C + 1, E1, HID])
        w1_hi = sb("w1_hi", [C + 1, E1 * HID], F32R)
        w1_lo = sb("w1_lo", [C + 1, E1 * HID], F32R)
        w2_f = sb("w2_f", [P, BLOCKS, C])
        b2_f = sb("b2_f", [65, E1 * C])
        b2_lead = sb("b2_lead", [65, 2, E1 * C], BF16)
        b2_rest = sb("b2_rest", [65, 2, E1 * C])
        b2_parts = sb("b2_parts", [C, E1 * C], BF16)
        X = sb("X", [P, IMAGES * TOKENS // P, C])
        XT = sb("XT", [C, IMAGES * TOKENS])
        gn_stats = sb("gn_stats", [C, IMAGES, 6])
        gn_mv = sb("gn_mv", [C, IMAGES, 2])
        gn_mean = sb("gn_mean", [C, IMAGES])
        gn_var = sb("gn_var", [C, IMAGES])
        gn_dev = sb("gn_dev", [C, IMAGES])
        gn_scale = sb("gn_scale", [C, IMAGES])
        gn_square = sb("gn_square", [C, IMAGES])
        gn_spread = sb("gn_spread", [C, IMAGES])
        gn_veps = sb("gn_veps", [C, IMAGES])
        xn = sb("xn", [C, PT])
        xn_hi = sb("xn_hi", [C + 1, PT], F32R)
        xn_lo = sb("xn_lo", [C + 1, PT], F32R)
        logit = sb("logit", [P, TILES, E0])
        gt0 = sb("gt0", [P, TILES, E0, E0])
        eq0 = sb("eq0", [P, TILES, E0, E0])
        rank0 = sb("rank0", [P, TILES, E0])
        chosen0 = sb("chosen0", [P, TILES, E0])
        picked0 = sb("picked0", [P, TILES, E0])
        sum0 = sb("sum0", [P, TILES])
        arg0 = sb("arg0", [P, TILES, E0])
        tanh0 = sb("tanh0", [P, TILES, E0])
        half0 = sb("half0", [P, TILES, E0])
        weight0 = sb("weight0", [P, TILES, E0])
        mixed = sb("mixed", [P, TILES, C])
        leaky = sb("leaky", [P, TILES, C])
        res1 = sb("res1", [P, TILES, C])
        res2 = sb("res2", [P, TILES, C])
        ln_stats = sb("ln_stats", [P, 2, TILES, 6])
        ln_mv = sb("ln_mv", [P, 2, TILES, 2])
        ln_var = sb("ln_var", [P, 2, TILES])
        ln_scale = sb("ln_scale", [P, 2, TILES])
        normed = sb("normed", [P, 2, TILES, C])
        t1_f = sb("t1_f", [C, PT])
        t1_hi = sb("t1_hi", [C, PT], F32R)
        t1_lo = sb("t1_lo", [C, PT], F32R)
        qk_parts = sb("qk_parts", [C, 2, 3, PT], BF16)
        qk_rest = sb("qk_rest", [C, 2, PT])
        q_stack = sb("q_stack", [STACK + SHIFT, HEADS, PT], BF16)
        k_stack = sb("k_stack", [STACK + SHIFT, HEADS, PT], BF16)
        v_aug = sb("v_aug", [P, TILES, HEADS, HS])
        row_max = sb("row_max", [P, TILES, HEADS])
        shift_parts = sb("shift_parts", [P, TILES, SHIFT, HEADS], BF16)
        shift_rest = sb("shift_rest", [P, TILES, HEADS])
        shift_t = sb("shift_t", [SHIFT * HEADS, PT], BF16)
        prob_a = sb("prob_a", [P, 2, HEADS, TOKENS])
        prob_b = sb("prob_b", [P, 2, HEADS, P])
        att_t = sb("att_t", [C, 2, 2, TOKENS])
        inv_sum = sb("inv_sum", [P, 2, 4 * HG])
        att = sb("att", [P, TILES, C])
        heads_t = sb("heads_t", [C + 1, PT])
        t2_f = sb("t2_f", [C + 1, PT])
        t2_hi = sb("t2_hi", [C + 1, PT], F32R)
        t2_lo = sb("t2_lo", [C + 1, PT], F32R)
        glogit = sb("glogit", [P, TILES, E1])
        gmax = sb("gmax", [P, TILES])
        gdiff = sb("gdiff", [P, TILES, E1])
        gexp = sb("gexp", [P, TILES, E1])
        gsum = sb("gsum", [P, TILES])
        ginv = sb("ginv", [P, TILES])
        gprob = sb("gprob", [P, TILES, E1])
        gt1 = sb("gt1", [P, TILES, E1, E1])
        eq1 = sb("eq1", [P, TILES, E1, E1])
        rank1 = sb("rank1", [P, TILES, E1])
        chosen1 = sb("chosen1", [P, TILES, E1])
        gpick = sb("gpick", [P, TILES, E1])
        gpsum = sb("gpsum", [P, TILES])
        gpeps = sb("gpeps", [P, TILES])
        gpinv = sb("gpinv", [P, TILES])
        weight1 = sb("weight1", [P, TILES, E1])
        hidden = sb("hidden", [P, BLOCKS, PT])
        result = sb("result", [P, TILES, C])

        x_loaded = [sem(f"x_loaded{n}") for n in range(X_LOADS)]
        w_loaded = sem("w_loaded")
        const_ready = sem("const_ready")
        zero_ready = sem("zero_ready")
        pad_ready = sem("pad_ready")
        gn_stat = sem("gn_stat")
        b2_step = sem("b2_step")
        split_hi = sem("split_hi")
        split_lo = sem("split_lo")
        xt_filled = sem("xt_filled")
        xt_copied = sem("xt_copied")
        gn_step = sem("gn_step")
        gn_averaged = sem("gn_averaged")
        gn_root = sem("gn_root")
        filled = sem("filled")
        act_drained = sem("act_drained")
        dve_drained = sem("dve_drained")
        dve_step = sem("dve_step")
        pool_step = sem("pool_step")
        xn_ready = sem("xn_ready")
        xn_hi_ready = sem("xn_hi_ready")
        xn_lo_ready = sem("xn_lo_ready")
        arg0_ready = sem("arg0_ready")
        tanh0_ready = sem("tanh0_ready")
        ln_ready = sem("ln_ready")
        normed_ready = sem("normed_ready")
        mid_ready = sem("mid_ready")
        low_ready = sem("low_ready")
        stacked = sem("stacked")
        shift_ready = sem("shift_ready")
        shift_placed = sem("shift_placed")
        prob_ready = sem("prob_ready")
        gdiff_ready = sem("gdiff_ready")
        gexp_ready = sem("gexp_ready")
        h_filled = sem("h_filled")
        h_ready = sem("h_ready")
        y_filled = sem("y_filled")
        y_mixed = sem("y_mixed")
        stored = sem("stored")

        N_FILL = len(FILLS)
        STACK_DMAS = 2 * len(K_PARTS)
        H_FREE, Y_FREE, STORE_FREE = 2, 8, 16

        def bank(fill):
            return 4 + FILLS.index(fill) % RING

        def drains(fill, engine):
            n = FILLS.index(fill) + 1
            return sum(engine in DRAINS[f[0]] for f in FILLS[:n])

        N_ACT = drains(FILLS[-1], "S")
        N_DVE = drains(FILLS[-1], "V")

        def wait_filled(eng, i, fill):
            eng.wait_ge(filled, at(i, N_FILL, FILLS.index(fill) + 1))

        def wait_act(eng, i, fill):
            eng.wait_ge(act_drained, at(i, N_ACT, drains(fill, "S")))

        def wait_dve(eng, i, fill):
            eng.wait_ge(dve_drained, at(i, N_DVE, drains(fill, "V")))

        def wait_bank_free(pe, i, fill):
            n = FILLS.index(fill)
            before = [m for m in range(N_FILL) if m % RING == n % RING and m < n]
            if not before:
                if isinstance(i, int) and i == 0:
                    return
                before = [m for m in range(N_FILL) if m % RING == n % RING]
                i = i - 1
            last = FILLS[before[-1]]
            if "S" in DRAINS[last[0]]:
                wait_act(pe, i, last)
            if "V" in DRAINS[last[0]]:
                wait_dve(pe, i, last)

        def pairs(eng, body):
            body(0, True, True, False)
            if ROLLED:
                with eng.Fori(1, PAIRS - 1) as i:
                    body(i, True, False, False)
            else:
                for i in range(1, PAIRS - 1):
                    body(i, True, False, False)
            body(PAIRS - 1, True, False, True)
            body(PAIRS, False, False, True)

        block = ctx.enter_context(nc.Block())

        @block.sync
        def _(sp):
            per = IMAGES * TOKENS // P // X_LOADS
            for n in range(X_LOADS):
                sp.dma_start(X[:, n * per:(n + 1) * per, :], x_t[:, n * per:(n + 1) * per, :]).then_inc(x_loaded[n], 16)

            sp.dma_start(w1_f[0:C, :, :], w1.rearrange("e c h -> c e h")).then_inc(w_loaded, 16)
            sp.dma_start(w2_f[:, :, :], w2.rearrange("e (k p) c -> p (e k) c", p=P)).then_inc(w_loaded, 16)

            def body(i, attn, first, last):
                for step in SCHEDULE:
                    if step[0] == "qk" and attn:
                        if not first:
                            wait_filled(sp, i - 1, ("prob", 1, 4))
                        for tensor, stack, parts in ((0, q_stack, Q_PARTS), (1, k_stack, K_PARTS)):
                            sp.wait_ge(low_ready, at(i, 2 * UNFUSED, (tensor + 1) * UNFUSED))
                            for n, part in enumerate(parts):
                                sp.dma_start(stack[n * D:(n + 1) * D, :, :], qk_parts[:, tensor, part, :]
                                             ).then_inc(stacked, 16)
                    elif step[0] == "shift" and attn:
                        wait_act(sp, i, step)
                        sp.dma_start(k_stack[STACK:STACK + SHIFT, :, :],
                                     shift_t[:, :]).then_inc(shift_placed, 16)
                    elif step == ("ffn2", E1 - 1) and not first:
                        f = i - 1
                        sp.wait_ge(y_mixed, at(f, E1 * TILES, E1 * TILES + Y_FREE))
                        sp.dma_start(out_t[:, bass.ds(f * TILES, TILES), :], result[:, :, :]).then_inc(stored, 16)

            sp.sem_inc(stored, STORE_FREE)
            pairs(sp, body)
            sp.wait_ge(stored, PAIRS * 16 + STORE_FREE)

        @block.gpsimd
        def _(pool):
            pool.memset(ones[:, :], 1.0).then_inc(zero_ready, 1)
            pool.memset(ident_b[:, :], 0.0).then_inc(zero_ready, 1)
            pool.memset(zeros_b[:, :], 0.0).then_inc(zero_ready, 1)
            pool.memset(group_avg[:, :], 1.0 / GC).then_inc(zero_ready, 1)
            pool.memset(ones_b[:, :], 1.0).then_inc(const_ready, 1)
            pool.memset(eps_t[:, :], 1e-5).then_inc(const_ready, 1)
            pool.memset(power_t[:, :], -0.5).then_inc(const_ready, 1)
            pool.wait_ge(zero_ready, 4)
            pool.affine_select(out=ident[:, :], in_=ones[:, :], compare_op=ALU.is_equal, fill=0.0, base=0,
                               pattern=[[-1, P]], channel_multiplier=1).then_inc(const_ready, 1)
            pool.affine_select(out=ident_b[:, :], in_=ident_b[:, :], compare_op=ALU.not_equal, fill=1.0, base=0,
                               pattern=[[-1, P]], channel_multiplier=1).then_inc(const_ready, 1)
            pool.affine_select(out=causal_b[:, :], in_=zeros_b[:, :], compare_op=ALU.is_ge, fill=MASKED, base=0,
                               pattern=[[-1, P]], channel_multiplier=1).then_inc(const_ready, 1)
            for before, n in ((before0, E0), (before1, E1)):
                pool.affine_select(out=before[:, :, :], in_=ones[:, 0:n * n].rearrange("p (e j) -> p e j", j=n),
                                   compare_op=ALU.is_gt, fill=0.0, base=0, pattern=[[1, n], [-1, n]],
                                   channel_multiplier=0).then_inc(const_ready, 1)
            g = group_avg[:, :].rearrange("p (g j) -> p g j", j=GC)
            pool.affine_select(out=g, in_=g, compare_op=ALU.is_ge, fill=0.0, base=0,
                               pattern=[[-GC, GROUPS], [0, GC]], channel_multiplier=1).then_inc(zero_ready, 1)
            pool.wait_ge(zero_ready, 5)
            pool.affine_select(out=g, in_=g, compare_op=ALU.is_ge, fill=0.0, base=GC - 1,
                               pattern=[[GC, GROUPS], [0, GC]], channel_multiplier=-1).then_inc(const_ready, 1)
            pool.wait_ge(const_ready, 9)
            pool.wait_ge(gn_step, 6)
            pool.tensor_tensor(gn_veps[:, :], gn_var[:, :], eps_t[0:C, 0:IMAGES], ALU.add).then_inc(gn_root, 1)
            pool.wait_ge(gn_root, 1)
            pool.tensor_tensor(gn_scale[:, :], gn_veps[:, :], power_t[0:C, 0:IMAGES], ALU.pow).then_inc(gn_root, 1)

            def layer_norm(i, which):
                pool.wait_ge(ln_ready, at(i, 2 * TILES * UNFUSED, TILES * (which + 1) * UNFUSED))
                s = 2 * which + 1
                pool.tensor_tensor(ln_var[:, which, :], ln_mv[:, which, :, 1], eps_t[:, 0:TILES], ALU.add
                                   ).then_inc(pool_step, 1)
                pool.wait_ge(pool_step, at(i, POOL_STEPS, s))
                pool.tensor_tensor(ln_scale[:, which, :], ln_var[:, which, :], power_t[:, 0:TILES], ALU.pow
                                   ).then_inc(pool_step, 1)
                pool.wait_ge(pool_step, at(i, POOL_STEPS, s + 1))
                source = (res1, res2)[which]
                if not (isinstance(i, int) and i == 0):
                    wait_filled(pool, i - 1, (("norm1_t",), ("norm2_t",))[which])
                for t in range(TILES):
                    pool.tensor_scalar(normed[:, which, t, :], source[:, t, :], ln_mv[:, which, t, 0:1],
                                       ln_scale[:, which, t:t + 1], ALU.subtract, ALU.mult
                                       ).then_inc(normed_ready, UNFUSED)

            def xn_rest(i):
                pool.wait_ge(xn_ready, at(i, 2, 2))
                pool.wait_ge(xn_hi_ready, at(i, 1, 1))
                if not (isinstance(i, int) and i == 0):
                    wait_filled(pool, i - 1, ("conv", TILES - 1))
                pool.tensor_tensor(xn_lo[0:C, :], xn[:, :], xn_hi[0:C, :].bitcast(F32), ALU.subtract
                                   ).then_inc(xn_lo_ready, 1)

            xn_rest(0)

            def body(i, attn, first, last):
                for step in SCHEDULE:
                    if not attn:
                        continue
                    if step[0] == "mix":
                        layer_norm(i, 0)
                    elif step[0] == "proj":
                        layer_norm(i, 1)
                    elif step[0] == "xn" and not last:
                        xn_rest(i + 1)
                    elif step[0] == "qk":
                        for tensor in range(2):
                            wait_dve(pool, i, ("q",) if tensor == 0 else ("k",))
                            if tensor == 0 and not first:
                                pool.wait_ge(stacked, at(i - 1, 16 * STACK_DMAS, 16 * STACK_DMAS))
                            pool.tensor_scalar(qk_parts[:, tensor, 1, :], qk_rest[:, tensor, :], 1.0, 0.0,
                                               ALU.mult, ALU.add).then_inc(mid_ready, UNFUSED)
                            pool.wait_ge(mid_ready, at(i, 2 * UNFUSED, (tensor + 1) * UNFUSED))
                            pool.tensor_tensor(qk_parts[:, tensor, 2, :], qk_rest[:, tensor, :],
                                               qk_parts[:, tensor, 1, :], ALU.subtract).then_inc(low_ready, UNFUSED)
                    elif step[0] == "prob" and step[2] in (2, 4):
                        b = step[1]
                        wait_act(pool, i, step)
                        block_ = prob_a[:, b, :, 0:P] if step[2] == 2 else prob_b[:, b, :, :]
                        pool.affine_select(out=block_, in_=block_, compare_op=ALU.is_ge, fill=0.0, base=0,
                                           pattern=[[0, HEADS], [1, P]], channel_multiplier=-1
                                           ).then_inc(prob_ready, UNFUSED)

            pairs(pool, body)

        @block.scalar
        def _(act):
            loads = [(conv_f[0:C, 0:E0 * C].rearrange("c (e d) -> c e d", d=C), conv_w.rearrange("e c d -> c e d")),
                     (conv_f[0:C, E0 * C:E0 * C + E0], conv_gate),
                     (conv_f[C:C + 1, 0:E0 * C], conv_b.rearrange("(a e) d -> a (e d)", a=1)),
                     (qk_f[:, 0, :, :], wq.rearrange("h c d -> c h d")),
                     (qk_f[:, 1, :, :], wk.rearrange("h c d -> c h d")),
                     (wv_f[:, :, :], wv.rearrange("h c d -> c h d")),
                     (wproj_f[0:C, :], wproj),
                     (wproj_f[C:C + 1, :], bproj.rearrange("(a n) -> a n", a=1)),
                     (gate_f[0:C, 0:E1], gate_w),
                     (gate_f[C:C + 1, 0:E1], gate_b.rearrange("(a n) -> a n", a=1)),
                     (w1_f[C:C + 1, :, :], b1.rearrange("(a e) h -> a e h", a=1))]
            loads += [(b2_f[r:r + 1, :], b2.rearrange("(a e) c -> a (e c)", a=1)) for r in (0, 32, 64)]
            act.wait_ge(pad_ready, 1)
            for dst, src in loads:
                act.dma_start(dst, src).then_inc(w_loaded, 16)

            for p in range(PAIRS):
                act.wait_ge(xt_filled, p + 1)
                act.activation(XT[:, p * PT:(p + 1) * PT], PS[0:C, p, :], ACT.Copy).then_inc(xt_copied, 1)
            act.wait_ge(w_loaded, 16 * (len(loads) + 2))
            act.wait_ge(pad_ready, 14)
            act.activation(conv_hi[:, :], conv_f[:, :], ACT.Copy).then_inc(split_hi, 1)
            for tensor in range(2):
                act.activation(qk_hi[:, tensor, :].rearrange("c (d h) -> c d h", h=HEADS),
                               qk_f[:, tensor, :, :].rearrange("c h d -> c d h"), ACT.Copy).then_inc(split_hi, 1)
            act.activation(w1_hi[:, :], w1_f[:, :, :].rearrange("c e h -> c (e h)"), ACT.Copy).then_inc(split_hi, 1)

            def xn_lead(i):
                act.wait_ge(xn_ready, at(i, 2, 2))
                if not (isinstance(i, int) and i == 0):
                    wait_filled(act, i - 1, ("conv", TILES - 1))
                act.activation(xn_hi[0:C, :], xn[:, :], ACT.Copy).then_inc(xn_hi_ready, 1)

            xn_lead(0)
            act.sem_inc(h_ready, H_FREE)

            def body(i, attn, first, last):
                f = i - 1
                for step in SCHEDULE:
                    kind = step[0]
                    if kind == "ffn1" and not first:
                        m = step[1]
                        if m == 0:
                            if not (isinstance(f, int) and f == 0):
                                wait_filled(act, f, ("gate2",))
                        act.wait_ge(h_filled, at(f, BLOCKS, m + 1))
                        act.activation(hidden[:, m, :], PS[:, m % 2, :], ACT.Gelu).then_inc(h_ready, 1)
                    if not attn:
                        continue
                    if kind == "gates":
                        act.wait_ge(arg0_ready, at(i, 1, 1))
                        act.activation(tanh0[:, :, :], arg0[:, :, :], ACT.Tanh).then_inc(tanh0_ready, 1)
                    elif kind == "norm1_t":
                        wait_filled(act, i, step)
                        ps = PS[0:C, bank(step), :]
                        act.activation(t1_f[:, :], ps, ACT.Copy)
                        act.activation(t1_hi[:, :], ps, ACT.Copy).then_inc(act_drained, 1)
                    elif kind == "qk":
                        for tensor, name in ((0, "q"), (1, "k")):
                            wait_filled(act, i, (name,))
                            if tensor == 0 and not first:
                                act.wait_ge(stacked, at(i - 1, 16 * STACK_DMAS, 16 * STACK_DMAS))
                            act.activation(qk_parts[:, tensor, 0, :], PS[0:C, bank((name,)), :], ACT.Copy
                                           ).then_inc(act_drained, 1)
                    elif kind == "v":
                        wait_filled(act, i, step)
                        act.activation(v_aug[:, :, :, 0:D],
                                       PS[:, bank(step), 0:TILES * C].rearrange("p (t h d) -> p t h d", h=HEADS, d=D),
                                       ACT.Copy).then_inc(act_drained, 1)
                    elif kind == "xn" and not last:
                        xn_lead(i + 1)
                    elif kind == "shift":
                        wait_filled(act, i, step)
                        if not first:
                            act.wait_ge(shift_placed, at(i - 1, 16, 16))
                        act.activation(shift_t[:, :], PS[0:SHIFT * HEADS, bank(step), 0:PT // 2].bitcast(BF16), ACT.Copy
                                       ).then_inc(act_drained, 1)
                    elif kind == "prob":
                        _, b, k = step
                        wait_filled(act, i, step)
                        if k == 0 and not first:
                            wait_filled(act, i - 1, ("pv", b))
                        if k < 3:
                            dst = prob_a[:, b, 2 * k:2 * k + 2, :].rearrange("p h t -> p (h t)")
                        else:
                            dst = prob_b[:, b, 4 * (k - 3):min(4 * (k - 3) + 4, HEADS), :].rearrange("p h t -> p (h t)")
                        act.activation(dst, PS[:, bank(step), 0:dst.shape[1]], ACT.Exp, scale=SCALE
                                       ).then_inc(act_drained, 1)
                    elif kind == "pv":
                        b = step[1]
                        wait_filled(act, i, step)
                        if not first:
                            wait_filled(act, i - 1, ("out_t", b))
                        act.activation(att_t[:, b, :, :].rearrange("p g t -> p (g t)"), PS[0:C, bank(step), :], ACT.Copy
                                       ).then_inc(act_drained, 1)
                    elif kind == "heads_t":
                        wait_filled(act, i, step)
                        act.activation(heads_t[0:C, :], PS[0:C, bank(step), :], ACT.Copy).then_inc(act_drained, 1)
                    elif kind == "norm2_t":
                        wait_filled(act, i, step)
                        ps = PS[0:C, bank(step), :]
                        act.activation(t2_f[0:C, :], ps, ACT.Copy)
                        act.activation(t2_hi[0:C, :], ps, ACT.Copy).then_inc(act_drained, 1)
                    elif kind == "gate2":
                        act.wait_ge(gdiff_ready, at(i, 1, 1))
                        act.activation(gexp[:, :, :], gdiff[:, :, :], ACT.Exp).then_inc(gexp_ready, 1)

            pairs(act, body)

        @block.tensor
        def _(pe):
            def split_product(dst, a_hi, a_lo, b_hi, b_lo):
                pe.matmul(dst, a_hi, b_hi, start=True, stop=False)
                pe.matmul(dst, a_hi, b_lo, start=False, stop=False)
                return pe.matmul(dst, a_lo, b_hi, start=False, stop=True)

            pe.wait_ge(const_ready, 9)
            for p in range(PAIRS):
                if p % (PAIRS // X_LOADS) == 0:
                    pe.wait_ge(x_loaded[p // (PAIRS // X_LOADS)], 16)
                for t in range(TILES):
                    last = pe.transpose(PS[0:C, p, t * P:(t + 1) * P], X[:, p * TILES + t, :], ident[:, :])
                last.then_inc(xt_filled, 1)
            pe.wait_ge(xt_copied, 1)
            pe.wait_ge(gn_step, 1)
            pe.matmul(PS[0:C, 0, 0:IMAGES], group_avg[:, :], gn_mv[:, :, 0], start=True, stop=True).then_inc(gn_averaged, 1)
            pe.wait_ge(gn_step, 5)
            pe.matmul(PS[0:C, 0, IMAGES:2 * IMAGES], group_avg[:, :], gn_spread[:, :], start=True, stop=True
                      ).then_inc(gn_averaged, 1)
            pe.wait_ge(split_lo, 3)
            pe.wait_ge(pad_ready, 14)
            pe.wait_ge(xt_copied, PAIRS)

            def body(i, attn, first, last):
                f = i - 1
                for step in SCHEDULE:
                    kind = step[0]
                    if kind == "ffn1" and not first:
                        m = step[1]
                        if m == 0:
                            wait_act(pe, f, ("norm2_t",))
                            wait_dve(pe, f, ("norm2_t",))
                        pe.wait_ge(h_ready, at(f, BLOCKS, m - 1 + H_FREE))
                        w = slice(m * P, (m + 1) * P)
                        split_product(PS[:, m % 2, :], w1_hi[:, w], w1_lo[:, w], t2_hi[:, :], t2_lo[:, :]
                                      ).then_inc(h_filled, 1)
                    elif kind == "ffn2" and not first:
                        e = step[1]
                        pe.wait_ge(h_ready, at(f, BLOCKS, CHUNKS * (e + 1) + H_FREE))
                        pe.wait_ge(y_mixed, at(f, E1 * TILES, TILES * (e - 1) + Y_FREE))
                        for t in range(TILES):
                            dst = PS[:, 2 + e % 2, t * C:(t + 1) * C]
                            pe.matmul(dst, ones_b[:, :], b2_parts[:, e * C:(e + 1) * C], start=True, stop=False)
                            for c in range(CHUNKS):
                                m = CHUNKS * e + c
                                mm = pe.matmul(dst, hidden[:, m, t * P:(t + 1) * P], w2_f[:, m, :],
                                               start=False, stop=c == CHUNKS - 1)
                        mm.then_inc(y_filled, 1)
                    if not attn:
                        continue
                    if kind == "conv":
                        pe.wait_ge(xn_hi_ready, at(i, 1, 1))
                        pe.wait_ge(xn_lo_ready, at(i, 1, 1))
                        for t in range(TILES):
                            wait_bank_free(pe, i, ("conv", t))
                            c = slice(t * P, (t + 1) * P)
                            split_product(PS[:, bank(("conv", t)), 0:CONV_N], xn_hi[:, c], xn_lo[:, c],
                                          conv_hi[:, :], conv_lo[:, :]).then_inc(filled, 1)
                    elif kind in ("norm1_t", "norm2_t"):
                        which = int(kind == "norm2_t")
                        wait_bank_free(pe, i, step)
                        pe.wait_ge(normed_ready, at(i, 2 * TILES * UNFUSED, TILES * (which + 1) * UNFUSED))
                        for t in range(TILES):
                            mm = pe.transpose(PS[0:C, bank(step), t * P:(t + 1) * P], normed[:, which, t, :], ident[:, :])
                        mm.then_inc(filled, 1)
                    elif kind == "qk":
                        wait_act(pe, i, ("norm1_t",))
                        wait_dve(pe, i, ("norm1_t",))
                        for tensor, name in ((0, "q"), (1, "k")):
                            wait_bank_free(pe, i, (name,))
                            split_product(PS[0:C, bank((name,)), :], qk_hi[:, tensor, :], qk_lo[:, tensor, :],
                                          t1_hi[:, :], t1_lo[:, :]).then_inc(filled, 1)
                    elif kind == "v":
                        wait_bank_free(pe, i, step)
                        for t in range(TILES):
                            mm = pe.matmul(PS[:, bank(step), t * C:(t + 1) * C], t1_f[:, t * P:(t + 1) * P],
                                           wv_f[:, :, :].rearrange("c h d -> c (h d)"), start=True, stop=True)
                        mm.then_inc(filled, 1)
                    elif kind == "score":
                        _, b, k = step
                        if (b, k) == (0, 0):
                            pe.wait_ge(stacked, at(i, 16 * STACK_DMAS, 16 * STACK_DMAS))
                        wait_bank_free(pe, i, step)
                        dst = PS[:, bank(step), :]
                        t0 = b * TOKENS
                        if k < 2:
                            heads = range(4 * k, min(4 * k + 4, HEADS))
                            n = len(heads)
                            pe.matmul(dst[:, 0:n * P], ident_b[:, :],
                                      causal_b[:, :].unsqueeze(1).to_broadcast([P, n, P]), start=True, stop=False,
                                      skip_group_check=True)
                            for j, h in enumerate(heads):
                                mm = pe.matmul(dst[:, j * P:(j + 1) * P], k_stack[0:STACK, h, t0:t0 + P],
                                               q_stack[0:STACK, h, t0:t0 + P], start=False, stop=j == n - 1,
                                               skip_group_check=True)
                        else:
                            heads = range(2 * (k - 2), 2 * (k - 2) + 2)
                            pe.matmul(dst.rearrange("p (h s) -> p h s", h=2)[:, :, P:TOKENS], ident_b[:, :],
                                      causal_b[:, :].unsqueeze(1).to_broadcast([P, 2, P]), start=True, stop=False,
                                      skip_group_check=True)
                            for j, h in enumerate(heads):
                                mm = pe.matmul(dst[:, j * TOKENS:(j + 1) * TOKENS], k_stack[0:STACK, h, t0 + P:t0 + TOKENS],
                                               q_stack[0:STACK, h, t0:t0 + TOKENS], start=False, stop=j == 1,
                                               skip_group_check=True)
                        mm.then_inc(filled, 1)
                    elif kind == "shift":
                        wait_bank_free(pe, i, step)
                        pe.wait_ge(shift_ready, at(i, 1, 1))
                        for t in range(TILES):
                            mm = pe.transpose(PS[0:SHIFT * HEADS, bank(step), t * P // 2:(t + 1) * P // 2].bitcast(BF16),
                                              shift_parts[:, t, :, :].rearrange("p a h -> p (a h)"), ident_b[:, :])
                        mm.then_inc(filled, 1)
                    elif kind == "prob":
                        _, b, k = step
                        if (b, k) == (0, 0):
                            pe.wait_ge(shift_placed, at(i, 16, 16))
                        wait_bank_free(pe, i, step)
                        dst = PS[:, bank(step), :]
                        t0 = b * TOKENS
                        if k < 3:
                            for j in range(2):
                                mm = pe.matmul(dst[:, j * TOKENS:(j + 1) * TOKENS], q_stack[:, 2 * k + j, t0:t0 + P],
                                               k_stack[:, 2 * k + j, t0:t0 + TOKENS], start=True, stop=True)
                        else:
                            for j, h in enumerate(range(4 * (k - 3), min(4 * (k - 3) + 4, HEADS))):
                                mm = pe.matmul(dst[:, j * P:(j + 1) * P], q_stack[:, h, t0 + P:t0 + TOKENS],
                                               k_stack[:, h, t0 + P:t0 + TOKENS], start=True, stop=True)
                        mm.then_inc(filled, 1)
                    elif kind == "pv":
                        b = step[1]
                        wait_bank_free(pe, i, step)
                        pe.wait_ge(prob_ready, at(i, 4 * UNFUSED, (2 * b + 2) * UNFUSED))
                        wait_act(pe, i, ("v",))
                        for g in range(2):
                            for half in range(2):
                                for j in range(HG):
                                    h = HG * g + j
                                    probs = prob_a[:, b, h, :] if half == 0 else prob_b[:, b, h, :]
                                    first_t = g * TOKENS + half * P
                                    mm = pe.matmul(PS[HS * j:HS * (j + 1), bank(step), first_t:(g + 1) * TOKENS],
                                                   v_aug[:, 2 * b + half, h, :], probs, start=half == 0, stop=half == 1,
                                                   skip_group_check=True)
                        mm.then_inc(filled, 1)
                    elif kind == "out_t":
                        b = step[1]
                        wait_bank_free(pe, i, step)
                        wait_act(pe, i, ("pv", b))
                        for t in range(2):
                            for g in range(2):
                                n = 2 * t + g
                                mm = pe.transpose(PS[:, bank(step), n * C:(n + 1) * C],
                                                  att_t[:, b, g, t * P:(t + 1) * P], ident[0:C, 0:C])
                        mm.then_inc(filled, 1)
                    elif kind == "heads_t":
                        wait_bank_free(pe, i, step)
                        wait_dve(pe, i, ("out_t", 1))
                        for t in range(TILES):
                            mm = pe.transpose(PS[0:C, bank(step), t * P:(t + 1) * P], att[:, t, :], ident[:, :])
                        mm.then_inc(filled, 1)
                    elif kind in ("proj", "gate2"):
                        lhs, rhs, source = (heads_t, wproj_f, "heads_t") if kind == "proj" else (t2_f, gate_f, "norm2_t")
                        wait_bank_free(pe, i, step)
                        wait_act(pe, i, (source,))
                        for t in range(TILES):
                            mm = pe.matmul(PS[:, bank(step), t * C:(t + 1) * C], lhs[:, t * P:(t + 1) * P], rhs[:, :],
                                           start=True, stop=True)
                        mm.then_inc(filled, 1)
                if first:
                    pe.wait_ge(split_lo, 7)

            pairs(pe, body)

        @block.vector
        def _(dve):
            def first_pair(i):
                return isinstance(i, int) and i == 0

            dve.memset(b2_f[:, :], 0.0).then_inc(pad_ready, 1)
            dve.memset(conv_f[:, CONV_N - 1:CONV_N], 0.0).then_inc(pad_ready, 1)
            dve.memset(conv_f[C:C + 1, E0 * C:CONV_N - 1], 0.0).then_inc(pad_ready, 1)
            dve.memset(gate_f[:, E1:C], 0.0).then_inc(pad_ready, 1)
            dve.memset(xn_hi[C:C + 1, :].bitcast(F32), 1.0).then_inc(pad_ready, 1)
            dve.memset(xn_lo[C:C + 1, :].bitcast(F32), 0.0).then_inc(pad_ready, 1)
            dve.memset(t2_hi[C:C + 1, :].bitcast(F32), 1.0).then_inc(pad_ready, 1)
            dve.memset(t2_lo[C:C + 1, :].bitcast(F32), 0.0).then_inc(pad_ready, 1)
            dve.memset(t2_f[C:C + 1, :], 1.0).then_inc(pad_ready, 1)
            dve.memset(heads_t[C:C + 1, :], 1.0).then_inc(pad_ready, 1)
            dve.memset(q_stack[STACK:STACK + SHIFT, :, :], 1.0).then_inc(pad_ready, 1)
            dve.memset(v_aug[:, :, :, D:D + 1], 1.0).then_inc(pad_ready, 1)
            dve.memset(v_aug[:, :, :, D + 1:HS], 0.0).then_inc(pad_ready, 1)
            dve.memset(b2_parts[:, :], 0.0).then_inc(pad_ready, 1)
            dve.sem_inc(y_mixed, Y_FREE)

            for n in range(IMAGES):
                dve.wait_ge(xt_copied, n // 2 + 1)
                dve.bn_stats(gn_stats[:, n, :], XT[:, n * TOKENS:(n + 1) * TOKENS]).then_inc(gn_stat, 1)
            for n in range(IMAGES):
                dve.wait_ge(gn_stat, n + 1)
                last = dve.bn_aggr(gn_mv[:, n, :], gn_stats[:, n, :])
            last.then_inc(gn_step, 1)
            dve.wait_ge(gn_averaged, 1)
            dve.tensor_copy(gn_mean[:, :], PS[0:C, 0, 0:IMAGES]).then_inc(gn_step, 1)
            dve.wait_ge(gn_step, 2)
            dve.tensor_tensor(gn_dev[:, :], gn_mv[:, :, 0], gn_mean[:, :], ALU.subtract).then_inc(gn_step, 1)
            dve.wait_ge(gn_step, 3)
            dve.tensor_tensor(gn_square[:, :], gn_dev[:, :], gn_dev[:, :], ALU.mult).then_inc(gn_step, 1)
            dve.wait_ge(gn_step, 4)
            dve.tensor_tensor(gn_spread[:, :], gn_square[:, :], gn_mv[:, :, 1], ALU.add).then_inc(gn_step, 1)
            dve.wait_ge(gn_averaged, 2)
            dve.tensor_copy(gn_var[:, :], PS[0:C, 0, IMAGES:2 * IMAGES]).then_inc(gn_step, 1)
            dve.wait_ge(split_hi, 1)
            dve.tensor_tensor(conv_lo[:, :], conv_f[:, :], conv_hi[:, :].bitcast(F32), ALU.subtract).then_inc(split_lo, 1)
            dve.wait_ge(split_hi, 3)
            for tensor in range(2):
                dve.tensor_tensor(qk_lo[:, tensor, :].rearrange("c (d h) -> c d h", h=HEADS),
                                  qk_f[:, tensor, :, :].rearrange("c h d -> c d h"),
                                  qk_hi[:, tensor, :].rearrange("c (d h) -> c d h", h=HEADS).bitcast(F32),
                                  ALU.subtract).then_inc(split_lo, 1)

            def normalise_x(i):
                if not first_pair(i):
                    dve.wait_ge(xn_hi_ready, at(i - 1, 1, 1))
                    dve.wait_ge(xn_lo_ready, at(i - 1, 1, 1))
                for b in range(2):
                    n = i * 2 + b
                    dve.tensor_scalar(xn[:, b * TOKENS:(b + 1) * TOKENS], XT[:, bass.ds(n * TOKENS, TOKENS)],
                                      gn_mean[:, bass.ds(n, 1)], gn_scale[:, bass.ds(n, 1)],
                                      ALU.subtract, ALU.mult).then_inc(xn_ready, 1)

            dve.wait_ge(gn_root, 2)
            normalise_x(0)
            dve.wait_ge(split_hi, 4)
            dve.tensor_tensor(w1_lo[:, :], w1_f[:, :, :].rearrange("c e h -> c (e h)"), w1_hi[:, :].bitcast(F32),
                              ALU.subtract).then_inc(split_lo, 1)
            dve.tensor_copy(b2_lead[:, 0, :], b2_f[:, :]).then_inc(b2_step, 1)
            dve.wait_ge(b2_step, 1)
            dve.tensor_tensor(b2_rest[:, 0, :], b2_f[:, :], b2_lead[:, 0, :], ALU.subtract).then_inc(b2_step, 1)
            dve.wait_ge(b2_step, 2)
            dve.tensor_copy(b2_lead[:, 1, :], b2_rest[:, 0, :]).then_inc(b2_step, 1)
            dve.wait_ge(b2_step, 3)
            dve.tensor_tensor(b2_rest[:, 1, :], b2_rest[:, 0, :], b2_lead[:, 1, :], ALU.subtract).then_inc(b2_step, 1)
            dve.tensor_copy(b2_parts[0:1, :], b2_lead[0:1, 0, :]).then_inc(split_lo, 1)
            dve.tensor_copy(b2_parts[32:33, :], b2_lead[32:33, 1, :]).then_inc(split_lo, 1)
            dve.wait_ge(b2_step, 4)
            dve.tensor_copy(b2_parts[64:65, :], b2_rest[64:65, 1, :]).then_inc(split_lo, 1)

            steps = 0

            def step_done(ins):
                nonlocal steps
                steps += 1
                ins.then_inc(dve_step, 1)

            def wait_step(i):
                dve.wait_ge(dve_step, at(i, DVE_STEPS, steps))

            def top_two(i, n, value, gt, eq, before, rank, chosen):
                shape = [P, TILES, n, n]
                of_j = value.unsqueeze(2).to_broadcast(shape)
                of_e = value.unsqueeze(3).to_broadcast(shape)
                step_done(dve.tensor_tensor(gt[:, :, :, :], of_j, of_e, ALU.is_gt))
                step_done(dve.tensor_tensor(eq[:, :, :, :], of_j, of_e, ALU.is_equal))
                wait_step(i)
                step_done(dve.tensor_tensor(eq[:, :, :, :], eq[:, :, :, :],
                                            before[:, :, :].unsqueeze(1).to_broadcast(shape), ALU.mult))
                wait_step(i)
                step_done(dve.tensor_tensor(gt[:, :, :, :], gt[:, :, :, :], eq[:, :, :, :], ALU.add))
                wait_step(i)
                step_done(dve.tensor_reduce(rank[:, :, :], gt[:, :, :, :], AX_X, ALU.add))
                wait_step(i)
                step_done(dve.tensor_scalar(chosen[:, :, :], rank[:, :, :], 1.5, None, ALU.is_lt))
                wait_step(i)

            def row_statistics(i, which, rows):
                base = steps
                for t in range(TILES):
                    step_done(dve.bn_stats(ln_stats[:, which, t, :], rows[:, t, :]))
                if not first_pair(i):
                    dve.wait_ge(normed_ready, at(i - 1, 2 * TILES * UNFUSED, TILES * (which + 1) * UNFUSED))
                for t in range(TILES):
                    dve.wait_ge(dve_step, at(i, DVE_STEPS, base + t + 1))
                    dve.bn_aggr(ln_mv[:, which, t, :], ln_stats[:, which, t, :]).then_inc(ln_ready, UNFUSED)

            def body(i, attn, first, last):
                nonlocal steps
                steps = 0
                f = i - 1
                for step in SCHEDULE:
                    kind = step[0]
                    if kind == "ffn2" and not first:
                        e = step[1]
                        dve.wait_ge(y_filled, at(f, E1, e + 1))
                        if e == 0:
                            dve.wait_ge(stored, at(f, 16, STORE_FREE))
                        for t in range(TILES):
                            dve.wait_ge(y_mixed, at(f, E1 * TILES, TILES * (e - 1) + t + 1 + Y_FREE))
                            dve.scalar_tensor_tensor(
                                result[:, t, :], PS[:, 2 + e % 2, t * C:(t + 1) * C], weight1[:, t, e:e + 1],
                                res2[:, t, :] if e == 0 else result[:, t, :], ALU.mult, ALU.add).then_inc(y_mixed, 1)
                    if not attn:
                        continue
                    if kind == "gates":
                        wait_filled(dve, i, ("conv", TILES - 1))
                        b0 = bank(("conv", 0))
                        step_done(dve.tensor_copy(logit[:, :, :], PS[:, b0:b0 + TILES, E0 * C:E0 * C + E0]))
                        wait_step(i)
                        top_two(i, E0, logit[:, :, :], gt0, eq0, before0, rank0, chosen0)
                        step_done(dve.tensor_tensor(picked0[:, :, :], chosen0[:, :, :], logit[:, :, :], ALU.mult))
                        wait_step(i)
                        step_done(dve.tensor_reduce(sum0[:, :], picked0[:, :, :], AX_X, ALU.add))
                        wait_step(i)
                        dve.scalar_tensor_tensor(arg0[:, :, :], sum0[:, :].unsqueeze(2).to_broadcast([P, TILES, E0]), -0.5,
                                                 logit[:, :, :], ALU.mult, ALU.add).then_inc(arg0_ready, 1)
                        dve.wait_ge(tanh0_ready, at(i, 1, 1))
                        step_done(dve.tensor_scalar(half0[:, :, :], tanh0[:, :, :], 0.5, 0.5, ALU.mult, ALU.add))
                        wait_step(i)
                        step_done(dve.tensor_tensor(weight0[:, :, :], half0[:, :, :], chosen0[:, :, :], ALU.mult))
                        wait_step(i)
                    elif kind == "mix":
                        base = steps
                        for e in range(E0):
                            for t in range(TILES):
                                y = PS[:, bank(("conv", t)), e * C:(e + 1) * C]
                                if e == 0:
                                    step_done(dve.tensor_scalar(mixed[:, t, :], y, weight0[:, t, 0:1], None, ALU.mult))
                                    continue
                                dve.wait_ge(dve_step, at(i, DVE_STEPS, base + TILES * (e - 1) + t + 1))
                                ins = dve.scalar_tensor_tensor(mixed[:, t, :], y, weight0[:, t, e:e + 1], mixed[:, t, :],
                                                               ALU.mult, ALU.add)
                                if e == E0 - 1:
                                    ins.then_inc(dve_drained, 1)
                                else:
                                    step_done(ins)
                        wait_dve(dve, i, ("conv", TILES - 1))
                        step_done(dve.scalar_tensor_tensor(leaky[:, :, :], mixed[:, :, :], 0.01, mixed[:, :, :],
                                                           ALU.mult, ALU.max))
                        wait_step(i)
                        if not first:
                            dve.wait_ge(normed_ready, at(i - 1, 2 * TILES * UNFUSED, TILES * UNFUSED))
                        step_done(dve.tensor_tensor(res1[:, :, :], leaky[:, :, :], X[:, bass.ds(i * TILES, TILES), :], ALU.add))
                        wait_step(i)
                        row_statistics(i, 0, res1)
                    elif kind in ("norm1_t", "norm2_t"):
                        lo, hi = (t1_lo, t1_hi) if kind == "norm1_t" else (t2_lo, t2_hi)
                        wait_filled(dve, i, step)
                        wait_act(dve, i, step)
                        dve.tensor_tensor(lo[0:C, :], PS[0:C, bank(step), :], hi[0:C, :].bitcast(F32), ALU.subtract
                                          ).then_inc(dve_drained, 1)
                    elif kind == "xn" and not last:
                        normalise_x(i + 1)
                    elif kind == "qk":
                        for tensor, name in ((0, "q"), (1, "k")):
                            wait_filled(dve, i, (name,))
                            wait_act(dve, i, (name,))
                            if not first:
                                dve.wait_ge(low_ready, at(i - 1, 2 * UNFUSED, (tensor + 1) * UNFUSED))
                            ins = dve.tensor_tensor(qk_rest[:, tensor, :], PS[0:C, bank((name,)), :],
                                                    qk_parts[:, tensor, 0, :], ALU.subtract)
                            ins.then_inc(dve_drained, 1)
                    elif kind == "score":
                        _, b, k = step
                        wait_filled(dve, i, step)
                        ps = PS[:, bank(step), :]
                        if k < 2:
                            n = min(4, HEADS - 4 * k)
                            dst, src = row_max[:, 2 * b, 4 * k:4 * k + n], ps[:, 0:n * P].rearrange("p (h s) -> p h s", s=P)
                        else:
                            dst = row_max[:, 2 * b + 1, 2 * (k - 2):2 * (k - 2) + 2]
                            src = ps.rearrange("p (h s) -> p h s", s=TOKENS)
                        dve.tensor_reduce(dst, src, AX_X, ALU.max).then_inc(dve_drained, 1)
                    elif kind == "shift":
                        wait_dve(dve, i, ("score", 1, 4))
                        if not first:
                            wait_filled(dve, i - 1, step)
                        lead = shift_parts[:, :, 0, :]
                        step_done(dve.tensor_scalar(lead, row_max[:, :, :], -1.0, None, ALU.mult))
                        wait_step(i)
                        step_done(dve.scalar_tensor_tensor(shift_rest[:, :, :], row_max[:, :, :], -1.0, lead,
                                                           ALU.mult, ALU.subtract))
                        wait_step(i)
                        step_done(dve.tensor_copy(shift_parts[:, :, 1, :], shift_rest[:, :, :]))
                        wait_step(i)
                        dve.tensor_tensor(shift_parts[:, :, 2, :], shift_rest[:, :, :], shift_parts[:, :, 1, :], ALU.subtract
                                          ).then_inc(shift_ready, 1)
                    elif kind == "out_t":
                        b = step[1]
                        wait_filled(dve, i, step)
                        rows = PS[:, bank(step), 0:4 * C].rearrange("p (n d) -> p n d", d=HS)
                        step_done(dve.reciprocal(inv_sum[:, b, :], rows[:, :, D]))
                        wait_step(i)
                        if b == 0 and not first:
                            wait_filled(dve, i - 1, ("heads_t",))
                        dve.tensor_tensor(att[:, 2 * b:2 * b + 2, :].rearrange("p t (h d) -> p (t h) d", d=D),
                                          rows[:, :, 0:D], inv_sum[:, b, :].unsqueeze(2).to_broadcast([P, 4 * HG, D]),
                                          ALU.mult).then_inc(dve_drained, 1)
                    elif kind == "proj":
                        wait_filled(dve, i, step)
                        if not first:
                            dve.wait_ge(y_mixed, at(f, E1 * TILES, TILES + Y_FREE))
                        dve.tensor_tensor(res2[:, :, :].rearrange("p t c -> p (t c)"), PS[:, bank(step), 0:TILES * C],
                                          res1[:, :, :].rearrange("p t c -> p (t c)"), ALU.add).then_inc(dve_drained, 1)
                        wait_dve(dve, i, step)
                        row_statistics(i, 1, res2)
                    elif kind == "gate2":
                        wait_filled(dve, i, step)
                        ps = PS[:, bank(step), 0:TILES * C].rearrange("p (t c) -> p t c", c=C)[:, :, 0:E1]
                        dve.tensor_copy(glogit[:, :, :], ps).then_inc(dve_drained, 1)
                        wait_dve(dve, i, step)
                        step_done(dve.tensor_reduce(gmax[:, :], glogit[:, :, :], AX_X, ALU.max))
                        wait_step(i)
                        wide = [P, TILES, E1]
                        dve.tensor_tensor(gdiff[:, :, :], glogit[:, :, :], gmax[:, :].unsqueeze(2).to_broadcast(wide),
                                          ALU.subtract).then_inc(gdiff_ready, 1)
                        dve.wait_ge(gexp_ready, at(i, 1, 1))
                        step_done(dve.tensor_reduce(gsum[:, :], gexp[:, :, :], AX_X, ALU.add))
                        wait_step(i)
                        step_done(dve.reciprocal(ginv[:, :], gsum[:, :]))
                        wait_step(i)
                        step_done(dve.tensor_tensor(gprob[:, :, :], gexp[:, :, :], ginv[:, :].unsqueeze(2).to_broadcast(wide),
                                                    ALU.mult))
                        wait_step(i)
                        top_two(i, E1, gprob[:, :, :], gt1, eq1, before1, rank1, chosen1)
                        step_done(dve.tensor_tensor(gpick[:, :, :], gprob[:, :, :], chosen1[:, :, :], ALU.mult))
                        wait_step(i)
                        step_done(dve.tensor_reduce(gpsum[:, :], gpick[:, :, :], AX_X, ALU.add))
                        wait_step(i)
                        step_done(dve.tensor_scalar(gpeps[:, :], gpsum[:, :], 1e-9, None, ALU.add))
                        wait_step(i)
                        step_done(dve.reciprocal(gpinv[:, :], gpeps[:, :]))
                        wait_step(i)
                        if not first:
                            dve.wait_ge(y_mixed, at(f, E1 * TILES, E1 * TILES + Y_FREE))
                        step_done(dve.tensor_tensor(weight1[:, :, :], gpick[:, :, :], gpinv[:, :].unsqueeze(2).to_broadcast(wide),
                                                    ALU.mult))
                        wait_step(i)
                assert not attn or steps == DVE_STEPS, steps

            pairs(dve, body)


_INS = ["x", "L0_conv_Wg", "L0_conv_We", "L0_conv_be", "L1_attn_wk", "L1_attn_wq", "L1_attn_wv", "L1_attn_wproj",
        "L1_attn_bproj", "L1_ffn_gate_w", "L1_ffn_gate_b", "L1_ffn_w1", "L1_ffn_b1", "L1_ffn_w2", "L1_ffn_b2"]
_OUTS = [((IMAGES, 16, 16, C), "float32")]


def kernel(**inputs):
    import numpy as _np
    import concourse.bacc as _bacc
    from concourse import mybir as _mybir
    from concourse.bass_utils import run_bass_kernel_spmd as _run

    nc = _bacc.Bacc("TRN2", target_bir_lowering=False, num_devices=1)
    arrays, args = {}, []
    for name in _INS:
        a = _np.ascontiguousarray(inputs[name])
        arrays[f"in_{name}_dram"] = a
        args.append(nc.dram_tensor(f"in_{name}_dram", a.shape, _mybir.dt.from_np(a.dtype), kind="ExternalInput").ap())
    for i, (shape, dtype) in enumerate(_OUTS):
        dt = _mybir.dt.from_np(_np.dtype(dtype))
        args.append(nc.dram_tensor(f"out_{i}_dram", shape, dt, kind="ExternalOutput").ap())
    build(nc, *args)
    r = _run(nc, [arrays], core_ids=[0])
    got = tuple(r.results[0][f"out_{i}_dram"] for i in range(len(_OUTS)))
    return got[0]
```

```python
from contextlib import ExitStack

import concourse.bass as bass
from concourse import mybir

ALU = mybir.AluOpType
ACT = mybir.ActivationFunctionType
AX_X = mybir.AxisListType.X
F32 = mybir.dt.float32
F32R = mybir.dt.float32r
BF16 = mybir.dt.bfloat16

P = 128
IMAGES, TOKENS, C = 16, 256, 96
GROUPS = 32
GC = C // GROUPS
E0 = 5
E1 = 4
HEADS, D = 6, 16
HID = 384
TILES = 4
PT = TILES * P
PAIRS = IMAGES * TOKENS // PT
CHUNKS = HID // P
BLOCKS = E1 * CHUNKS
HG = 3
HS = 32
CONV_N = E0 * C + E0 + 1
SCALE = float(C) ** -0.5
MASKED = -1.0e30
K_PARTS = (0, 0, 1, 0, 2, 1)
Q_PARTS = (0, 1, 0, 2, 0, 1)
STACK = len(K_PARTS) * D
SHIFT = 3
X_LOADS = 4

FRONT, ATTN, FFN = 0, 1, 2
STAGES = (FRONT, ATTN, FFN)
STAGE_OF = {"xn": FRONT, "conv": FRONT, "gates": FRONT, "mix": FRONT, "norm1": FRONT, "norm1_t": FRONT,
            "qk": FRONT, "v": FRONT, "hold": FRONT,
            "score": ATTN, "shift": ATTN, "prob": ATTN, "pv": ATTN, "out_t": ATTN, "heads_t": ATTN, "proj": ATTN,
            "norm2": ATTN, "norm2_t": ATTN, "gate2": ATTN,
            "weights": FFN, "ffn1": FFN, "ffn2": FFN}
SCHEDULE = (
    [("xn",), ("ffn1", 0), ("score", 0, 0), ("score", 0, 1), ("score", 0, 2), ("ffn1", 1), ("score", 0, 3),
     ("score", 0, 4), ("ffn1", 2), ("conv",), ("score", 1, 0), ("score", 1, 1), ("ffn1", 3), ("score", 1, 2),
     ("ffn1", 4), ("score", 1, 3), ("ffn1", 5), ("score", 1, 4), ("ffn1", 6), ("shift",), ("gates",)]
    + [("ffn1", m) for m in range(7, BLOCKS)] + [("weights",)]
    + [("prob", 0, k) for k in range(5)] + [("ffn2", 0), ("prob", 1, 0), ("prob", 1, 1), ("pv", 0)]
    + [("prob", 1, k) for k in range(2, 5)]
    + [("mix",), ("norm1",), ("ffn2", 1), ("out_t", 0), ("pv", 1), ("out_t", 1), ("norm1_t",), ("heads_t",),
       ("qk",), ("proj",), ("ffn2", 2), ("norm2",), ("v",), ("hold",), ("ffn2", 3), ("norm2_t",), ("gate2",)]
)
assert SCHEDULE.index(("ffn1", BLOCKS - 1)) < SCHEDULE.index(("norm2_t",))

HIDDEN_BANKS = (0, 1)
Y_BANK = 2
RING = {FRONT: (3, 4), ATTN: (5, 6, 7)}
UNFUSED = 2
DRAINS = {"conv": "S", "norm1_t": "SV", "q": "SV", "k": "SV", "v": "S", "score": "V", "shift": "S",
          "prob": "S", "pv": "S", "out_t": "V", "heads_t": "S", "proj": "V", "norm2_t": "SV", "gate2": "V"}
FILL_STAGE = dict(STAGE_OF, q=FRONT, k=FRONT)


def list_fills(stage):
    fills = []
    for step in SCHEDULE:
        if STAGE_OF[step[0]] != stage:
            continue
        if step[0] == "conv":
            fills += [("conv", t) for t in range(TILES)]
        elif step[0] == "qk":
            fills += [("q",), ("k",)]
        elif step[0] in DRAINS:
            fills.append(step)
    return fills


FILLS = {stage: list_fills(stage) for stage in RING}
DVE_STEPS = {FRONT: 35, ATTN: 10, FFN: 14}


def at(i, per, n):
    return i * per + n


def build(nc, x, conv_gate, conv_w, conv_b, wk, wq, wv, wproj, bproj, gate_w, gate_b, w1, b1, w2, b2, out):
    x_t = x.rearrange("b h w c -> (b h w) c").rearrange("(t p) c -> p t c", p=P)
    out_t = out.rearrange("b h w c -> (b h w) c").rearrange("(t p) c -> p t c", p=P)

    with ExitStack() as ctx:
        def sb(name, shape, dt=F32):
            return ctx.enter_context(nc.sbuf_tensor(name, shape, dt))

        def sem(name):
            return ctx.enter_context(nc.semaphore(name))

        PS = ctx.enter_context(nc.psum_tensor("PS", [P, 8, 512], F32))

        ones = sb("ones", [P, P])
        ident = sb("ident", [P, P])
        ident_b = sb("ident_b", [P, P], BF16)
        zeros_b = sb("zeros_b", [P, P], BF16)
        causal_b = sb("causal_b", [P, P], BF16)
        group_avg = sb("group_avg", [C, C])
        ones_b = sb("ones_b", [C, P], BF16)
        before0 = sb("before0", [P, E0, E0])
        before1 = sb("before1", [P, E1, E1])
        eps_t = sb("eps_t", [P, 32])
        power_t = sb("power_t", [P, 32])
        conv_f = sb("conv_f", [C + 1, CONV_N])
        conv_hi = sb("conv_hi", [C + 1, CONV_N], F32R)
        conv_lo = sb("conv_lo", [C + 1, CONV_N], F32R)
        qk_f = sb("qk_f", [C, 2, HEADS, D])
        qk_hi = sb("qk_hi", [C, 2, C], F32R)
        qk_lo = sb("qk_lo", [C, 2, C], F32R)
        wv_f = sb("wv_f", [C, HEADS, D])
        wproj_f = sb("wproj_f", [C + 1, C])
        gate_f = sb("gate_f", [C + 1, C])
        w1_f = sb("w1_f", [C + 1, E1, HID])
        w1_hi = sb("w1_hi", [C + 1, E1 * HID], F32R)
        w1_lo = sb("w1_lo", [C + 1, E1 * HID], F32R)
        w2_f = sb("w2_f", [P, BLOCKS, C])
        b2_f = sb("b2_f", [65, E1 * C])
        b2_lead = sb("b2_lead", [65, 2, E1 * C], BF16)
        b2_rest = sb("b2_rest", [65, 2, E1 * C])
        b2_parts = sb("b2_parts", [C, E1 * C], BF16)
        X = sb("X", [P, IMAGES * TOKENS // P, C])
        XT = sb("XT", [C, IMAGES * TOKENS])
        gn_stats = sb("gn_stats", [C, IMAGES, 6])
        gn_mv = sb("gn_mv", [C, IMAGES, 2])
        gn_mean = sb("gn_mean", [C, IMAGES])
        gn_var = sb("gn_var", [C, IMAGES])
        gn_dev = sb("gn_dev", [C, IMAGES])
        gn_scale = sb("gn_scale", [C, IMAGES])
        gn_square = sb("gn_square", [C, IMAGES])
        gn_spread = sb("gn_spread", [C, IMAGES])
        gn_veps = sb("gn_veps", [C, IMAGES])
        xn = sb("xn", [C, PT])
        xn_hi = sb("xn_hi", [C + 1, PT], F32R)
        xn_lo = sb("xn_lo", [C + 1, PT], F32R)
        conv_y = sb("conv_y", [P, TILES, CONV_N])
        gt0 = sb("gt0", [P, TILES, E0, E0])
        eq0 = sb("eq0", [P, TILES, E0, E0])
        rank0 = sb("rank0", [P, TILES, E0])
        chosen0 = sb("chosen0", [P, TILES, E0])
        picked0 = sb("picked0", [P, TILES, E0])
        sum0 = sb("sum0", [P, TILES])
        arg0 = sb("arg0", [P, TILES, E0])
        tanh0 = sb("tanh0", [P, TILES, E0])
        half0 = sb("half0", [P, TILES, E0])
        weight0 = sb("weight0", [P, TILES, E0])
        mixed = sb("mixed", [P, TILES, C])
        leaky = sb("leaky", [P, TILES, C])
        res1 = sb("res1", [P, TILES, C])
        held = sb("held", [P, TILES, C])
        res2 = sb("res2", [P, TILES, C])
        ln_stats = sb("ln_stats", [P, 2, TILES, 6])
        ln_mv = sb("ln_mv", [P, 2, TILES, 2])
        ln_var = sb("ln_var", [P, 2, TILES])
        ln_scale = sb("ln_scale", [P, 2, TILES])
        normed = sb("normed", [P, 2, TILES, C])
        t1_f = sb("t1_f", [C, PT])
        t1_hi = sb("t1_hi", [C, PT], F32R)
        t1_lo = sb("t1_lo", [C, PT], F32R)
        qk_parts = sb("qk_parts", [C, 2, 3, PT], BF16)
        qk_rest = sb("qk_rest", [C, 2, PT])
        q_stack = sb("q_stack", [STACK + SHIFT, HEADS, PT], BF16)
        k_stack = sb("k_stack", [STACK + SHIFT, HEADS, PT], BF16)
        v_aug = sb("v_aug", [P, TILES, HEADS, HS])
        row_max = sb("row_max", [P, TILES, HEADS])
        shift_parts = sb("shift_parts", [P, TILES, SHIFT, HEADS], BF16)
        shift_rest = sb("shift_rest", [P, TILES, HEADS])
        shift_t = sb("shift_t", [SHIFT * HEADS, PT], BF16)
        prob_a = sb("prob_a", [P, 2, HEADS, TOKENS])
        prob_b = sb("prob_b", [P, 2, HEADS, P])
        att_t = sb("att_t", [C, 2, 2, TOKENS])
        inv_sum = sb("inv_sum", [P, 2, 4 * HG])
        att = sb("att", [P, TILES, C])
        heads_t = sb("heads_t", [C + 1, PT])
        t2_f = sb("t2_f", [C + 1, PT])
        t2_hi = sb("t2_hi", [C + 1, PT], F32R)
        t2_lo = sb("t2_lo", [C + 1, PT], F32R)
        glogit = sb("glogit", [P, TILES, E1])
        gmax = sb("gmax", [P, TILES])
        gdiff = sb("gdiff", [P, TILES, E1])
        gexp = sb("gexp", [P, TILES, E1])
        gsum = sb("gsum", [P, TILES])
        ginv = sb("ginv", [P, TILES])
        gprob = sb("gprob", [P, TILES, E1])
        gt1 = sb("gt1", [P, TILES, E1, E1])
        eq1 = sb("eq1", [P, TILES, E1, E1])
        rank1 = sb("rank1", [P, TILES, E1])
        chosen1 = sb("chosen1", [P, TILES, E1])
        gpick = sb("gpick", [P, TILES, E1])
        gpsum = sb("gpsum", [P, TILES])
        gpeps = sb("gpeps", [P, TILES])
        gpinv = sb("gpinv", [P, TILES])
        weight1 = sb("weight1", [P, TILES, E1])
        hidden = sb("hidden", [P, BLOCKS, PT])
        result = sb("result", [P, TILES, C])

        x_loaded = [sem(f"x_loaded{n}") for n in range(X_LOADS)]
        w_loaded = sem("w_loaded")
        const_ready = sem("const_ready")
        zero_ready = sem("zero_ready")
        pad_ready = sem("pad_ready")
        gn_stat = sem("gn_stat")
        b2_step = sem("b2_step")
        split_hi = sem("split_hi")
        split_lo = sem("split_lo")
        xt_filled = sem("xt_filled")
        xt_copied = sem("xt_copied")
        gn_step = sem("gn_step")
        gn_averaged = sem("gn_averaged")
        gn_root = sem("gn_root")
        names = {FRONT: "front", ATTN: "attn", FFN: "ffn"}
        filled = {g: sem(f"filled_{names[g]}") for g in RING}
        act_drained = {g: sem(f"act_drained_{names[g]}") for g in RING}
        dve_drained = {g: sem(f"dve_drained_{names[g]}") for g in RING}
        dve_step = {g: sem(f"dve_step_{names[g]}") for g in STAGES}
        ln_step = [sem(f"ln_step{n}") for n in range(2)]
        ln_ready = [sem(f"ln_ready{n}") for n in range(2)]
        rstd_ready = [sem(f"rstd_ready{n}") for n in range(2)]
        normed_ready = [sem(f"normed_ready{n}") for n in range(2)]
        held_ready = sem("held_ready")
        res_ready = sem("res_ready")
        xn_ready = sem("xn_ready")
        xn_hi_ready = sem("xn_hi_ready")
        xn_lo_ready = sem("xn_lo_ready")
        arg0_ready = sem("arg0_ready")
        tanh0_ready = sem("tanh0_ready")
        mid_ready = sem("mid_ready")
        low_ready = sem("low_ready")
        stacked = sem("stacked")
        shift_ready = sem("shift_ready")
        shift_placed = sem("shift_placed")
        prob_ready = sem("prob_ready")
        gdiff_ready = sem("gdiff_ready")
        gexp_ready = sem("gexp_ready")
        h_filled = sem("h_filled")
        h_ready = sem("h_ready")
        y_filled = sem("y_filled")
        y_mixed = sem("y_mixed")
        stored = sem("stored")

        STACK_DMAS = 2 * len(K_PARTS)
        H_FREE, Y_FREE, STORE_FREE, HIDDEN_FREE = 2, TILES, 16, 1

        def bank(fill):
            ring = RING[FILL_STAGE[fill[0]]]
            return ring[FILLS[FILL_STAGE[fill[0]]].index(fill) % len(ring)]

        def drains(fill, engine):
            fills = FILLS[FILL_STAGE[fill[0]]]
            return sum(engine in DRAINS[f[0]] for f in fills[:fills.index(fill) + 1])

        def wait_filled(eng, n, fill):
            g = FILL_STAGE[fill[0]]
            eng.wait_ge(filled[g], at(n, len(FILLS[g]), FILLS[g].index(fill) + 1))

        def wait_act(eng, n, fill):
            g = FILL_STAGE[fill[0]]
            eng.wait_ge(act_drained[g], at(n, drains(FILLS[g][-1], "S"), drains(fill, "S")))

        def wait_dve(eng, n, fill):
            g = FILL_STAGE[fill[0]]
            eng.wait_ge(dve_drained[g], at(n, drains(FILLS[g][-1], "V"), drains(fill, "V")))

        def is_first(n):
            return isinstance(n, int) and n == 0

        def wait_bank_free(pe, n, fill):
            fills = FILLS[FILL_STAGE[fill[0]]]
            k = fills.index(fill)
            same = [m for m in range(len(fills)) if bank(fills[m]) == bank(fill)]
            before = [m for m in same if m < k]
            if not before:
                if is_first(n):
                    return
                before, n = same, n - 1
            last = fills[before[-1]]
            if "S" in DRAINS[last[0]]:
                wait_act(pe, n, last)
            if "V" in DRAINS[last[0]]:
                wait_dve(pe, n, last)

        def iterations(eng, body):
            body(0, (FRONT,))
            body(1, (FRONT, ATTN))
            with eng.Fori(2, PAIRS) as i:
                body(i, STAGES)
            body(PAIRS, (ATTN, FFN))
            body(PAIRS + 1, (FFN,))

        def steps_of(i, stages):
            for step in SCHEDULE:
                stage = STAGE_OF[step[0]]
                if stage in stages:
                    yield step, step[0], i - stage if stage else i

        block = ctx.enter_context(nc.Block())

        @block.sync
        def _(sp):
            per = IMAGES * TOKENS // P // X_LOADS
            for n in range(X_LOADS):
                sp.dma_start(X[:, n * per:(n + 1) * per, :], x_t[:, n * per:(n + 1) * per, :]).then_inc(x_loaded[n], 16)

            sp.dma_start(w1_f[0:C, :, :], w1.rearrange("e c h -> c e h")).then_inc(w_loaded, 16)
            sp.dma_start(w2_f[:, :, :], w2.rearrange("e (k p) c -> p (e k) c", p=P)).then_inc(w_loaded, 16)

            def body(i, stages):
                for step, kind, n in steps_of(i, stages):
                    if kind == "qk":
                        if not is_first(n):
                            wait_filled(sp, n - 1, ("prob", 1, 4))
                        for tensor, stack, parts in ((0, q_stack, Q_PARTS), (1, k_stack, K_PARTS)):
                            sp.wait_ge(low_ready, at(n, 2 * UNFUSED, (tensor + 1) * UNFUSED))
                            for r, part in enumerate(parts):
                                sp.dma_start(stack[r * D:(r + 1) * D, :, :], qk_parts[:, tensor, part, :]
                                             ).then_inc(stacked, 16)
                    elif kind == "shift":
                        wait_act(sp, n, step)
                        sp.dma_start(k_stack[STACK:STACK + SHIFT, :, :],
                                     shift_t[:, :]).then_inc(shift_placed, 16)
                    elif step == ("ffn2", E1 - 1):
                        sp.wait_ge(y_mixed, at(n, E1 * TILES, E1 * TILES + Y_FREE))
                        sp.dma_start(out_t[:, bass.ds(n * TILES, TILES), :], result[:, :, :]).then_inc(stored, 16)

            sp.sem_inc(stored, STORE_FREE)
            iterations(sp, body)
            sp.wait_ge(stored, PAIRS * 16 + STORE_FREE)

        @block.gpsimd
        def _(pool):
            pool.memset(ones[:, :], 1.0).then_inc(zero_ready, 1)
            pool.memset(ident_b[:, :], 0.0).then_inc(zero_ready, 1)
            pool.memset(zeros_b[:, :], 0.0).then_inc(zero_ready, 1)
            pool.memset(group_avg[:, :], 1.0 / GC).then_inc(zero_ready, 1)
            pool.memset(ones_b[:, :], 1.0).then_inc(const_ready, 1)
            pool.memset(eps_t[:, :], 1e-5).then_inc(const_ready, 1)
            pool.memset(power_t[:, :], -0.5).then_inc(const_ready, 1)
            pool.wait_ge(zero_ready, 4)
            pool.affine_select(out=ident[:, :], in_=ones[:, :], compare_op=ALU.is_equal, fill=0.0, base=0,
                               pattern=[[-1, P]], channel_multiplier=1).then_inc(const_ready, 1)
            pool.affine_select(out=ident_b[:, :], in_=ident_b[:, :], compare_op=ALU.not_equal, fill=1.0, base=0,
                               pattern=[[-1, P]], channel_multiplier=1).then_inc(const_ready, 1)
            pool.affine_select(out=causal_b[:, :], in_=zeros_b[:, :], compare_op=ALU.is_ge, fill=MASKED, base=0,
                               pattern=[[-1, P]], channel_multiplier=1).then_inc(const_ready, 1)
            for before, n in ((before0, E0), (before1, E1)):
                pool.affine_select(out=before[:, :, :], in_=ones[:, 0:n * n].rearrange("p (e j) -> p e j", j=n),
                                   compare_op=ALU.is_gt, fill=0.0, base=0, pattern=[[1, n], [-1, n]],
                                   channel_multiplier=0).then_inc(const_ready, 1)
            g = group_avg[:, :].rearrange("p (g j) -> p g j", j=GC)
            pool.affine_select(out=g, in_=g, compare_op=ALU.is_ge, fill=0.0, base=0,
                               pattern=[[-GC, GROUPS], [0, GC]], channel_multiplier=1).then_inc(zero_ready, 1)
            pool.wait_ge(zero_ready, 5)
            pool.affine_select(out=g, in_=g, compare_op=ALU.is_ge, fill=0.0, base=GC - 1,
                               pattern=[[GC, GROUPS], [0, GC]], channel_multiplier=-1).then_inc(const_ready, 1)
            pool.wait_ge(const_ready, 9)
            pool.wait_ge(gn_step, 6)
            pool.tensor_tensor(gn_veps[:, :], gn_var[:, :], eps_t[0:C, 0:IMAGES], ALU.add).then_inc(gn_root, 1)
            pool.wait_ge(gn_root, 1)
            pool.tensor_tensor(gn_scale[:, :], gn_veps[:, :], power_t[0:C, 0:IMAGES], ALU.pow).then_inc(gn_root, 1)

            def inverse_root(n, which):
                pool.wait_ge(ln_ready[which], at(n, TILES * UNFUSED, TILES * UNFUSED))
                pool.tensor_tensor(ln_var[:, which, :], ln_mv[:, which, :, 1], eps_t[:, 0:TILES], ALU.add
                                   ).then_inc(ln_step[which], 1)
                pool.wait_ge(ln_step[which], at(n, 1, 1))
                pool.tensor_tensor(ln_scale[:, which, :], ln_var[:, which, :], power_t[:, 0:TILES], ALU.pow
                                   ).then_inc(rstd_ready[which], 1)

            def body(i, stages):
                for step, kind, n in steps_of(i, stages):
                    if kind == "norm1":
                        inverse_root(n, 0)
                    elif kind == "norm2":
                        inverse_root(n, 1)
                    elif kind == "xn":
                        pool.wait_ge(xn_ready, at(n, 2, 2))
                        pool.wait_ge(xn_hi_ready, at(n, 1, 1))
                        if not is_first(n):
                            wait_filled(pool, n - 1, ("conv", TILES - 1))
                        pool.tensor_tensor(xn_lo[0:C, :], xn[:, :], xn_hi[0:C, :].bitcast(F32), ALU.subtract
                                           ).then_inc(xn_lo_ready, 1)
                    elif kind == "qk":
                        for tensor in range(2):
                            wait_dve(pool, n, ("q",) if tensor == 0 else ("k",))
                            if tensor == 0 and not is_first(n):
                                pool.wait_ge(stacked, at(n - 1, 16 * STACK_DMAS, 16 * STACK_DMAS))
                            pool.tensor_scalar(qk_parts[:, tensor, 1, :], qk_rest[:, tensor, :], 1.0, 0.0,
                                               ALU.mult, ALU.add).then_inc(mid_ready, UNFUSED)
                            pool.wait_ge(mid_ready, at(n, 2 * UNFUSED, (tensor + 1) * UNFUSED))
                            pool.tensor_tensor(qk_parts[:, tensor, 2, :], qk_rest[:, tensor, :],
                                               qk_parts[:, tensor, 1, :], ALU.subtract).then_inc(low_ready, UNFUSED)
                    elif kind == "hold":
                        pool.wait_ge(res_ready, at(n, 1, 1))
                        if not is_first(n):
                            wait_dve(pool, n - 1, ("proj",))
                        pool.tensor_scalar(held[:, :, :], res1[:, :, :], 1.0, 0.0, ALU.mult, ALU.add
                                           ).then_inc(held_ready, UNFUSED)
                    elif kind == "prob" and step[2] in (2, 4):
                        b = step[1]
                        wait_act(pool, n, step)
                        block_ = prob_a[:, b, :, 0:P] if step[2] == 2 else prob_b[:, b, :, :]
                        pool.affine_select(out=block_, in_=block_, compare_op=ALU.is_ge, fill=0.0, base=0,
                                           pattern=[[0, HEADS], [1, P]], channel_multiplier=-1
                                           ).then_inc(prob_ready, UNFUSED)

            iterations(pool, body)

        @block.scalar
        def _(act):
            loads = [(conv_f[0:C, 0:E0 * C].rearrange("c (e d) -> c e d", d=C), conv_w.rearrange("e c d -> c e d")),
                     (conv_f[0:C, E0 * C:E0 * C + E0], conv_gate),
                     (conv_f[C:C + 1, 0:E0 * C], conv_b.rearrange("(a e) d -> a (e d)", a=1)),
                     (qk_f[:, 0, :, :], wq.rearrange("h c d -> c h d")),
                     (qk_f[:, 1, :, :], wk.rearrange("h c d -> c h d")),
                     (wv_f[:, :, :], wv.rearrange("h c d -> c h d")),
                     (wproj_f[0:C, :], wproj),
                     (wproj_f[C:C + 1, :], bproj.rearrange("(a n) -> a n", a=1)),
                     (gate_f[0:C, 0:E1], gate_w),
                     (gate_f[C:C + 1, 0:E1], gate_b.rearrange("(a n) -> a n", a=1)),
                     (w1_f[C:C + 1, :, :], b1.rearrange("(a e) h -> a e h", a=1))]
            loads += [(b2_f[r:r + 1, :], b2.rearrange("(a e) c -> a (e c)", a=1)) for r in (0, 32, 64)]
            act.wait_ge(pad_ready, 1)
            for dst, src in loads:
                act.dma_start(dst, src).then_inc(w_loaded, 16)

            for p in range(PAIRS):
                act.wait_ge(xt_filled, p + 1)
                act.activation(XT[:, p * PT:(p + 1) * PT], PS[0:C, p, :], ACT.Copy).then_inc(xt_copied, 1)
            act.wait_ge(w_loaded, 16 * (len(loads) + 2))
            act.wait_ge(pad_ready, 14)
            act.activation(conv_hi[:, :], conv_f[:, :], ACT.Copy).then_inc(split_hi, 1)
            for tensor in range(2):
                act.activation(qk_hi[:, tensor, :].rearrange("c (d h) -> c d h", h=HEADS),
                               qk_f[:, tensor, :, :].rearrange("c h d -> c d h"), ACT.Copy).then_inc(split_hi, 1)
            act.activation(w1_hi[:, :], w1_f[:, :, :].rearrange("c e h -> c (e h)"), ACT.Copy).then_inc(split_hi, 1)

            act.sem_inc(h_ready, H_FREE)

            def body(i, stages):
                for step, kind, n in steps_of(i, stages):
                    first = is_first(n)
                    if kind == "ffn1":
                        m = step[1]
                        if m == 0:
                            act.wait_ge(y_filled, at(n, E1, HIDDEN_FREE))
                        act.wait_ge(h_filled, at(n, BLOCKS, m + 1))
                        act.activation(hidden[:, m, :], PS[:, HIDDEN_BANKS[m % 2], :], ACT.Gelu).then_inc(h_ready, 1)
                    elif kind == "xn":
                        act.wait_ge(xn_ready, at(n, 2, 2))
                        if not first:
                            wait_filled(act, n - 1, ("conv", TILES - 1))
                        act.activation(xn_hi[0:C, :], xn[:, :], ACT.Copy).then_inc(xn_hi_ready, 1)
                    elif kind == "conv":
                        if not first:
                            act.wait_ge(res_ready, at(n - 1, 1, 1))
                        for t in range(TILES):
                            wait_filled(act, n, ("conv", t))
                            act.activation(conv_y[:, t, :], PS[:, bank(("conv", t)), 0:CONV_N], ACT.Copy
                                           ).then_inc(act_drained[FRONT], 1)
                    elif kind == "gates":
                        act.wait_ge(arg0_ready, at(n, 1, 1))
                        act.activation(tanh0[:, :, :], arg0[:, :, :], ACT.Tanh).then_inc(tanh0_ready, 1)
                    elif kind == "norm1_t":
                        wait_filled(act, n, step)
                        ps = PS[0:C, bank(step), :]
                        act.activation(t1_f[:, :], ps, ACT.Copy)
                        act.activation(t1_hi[:, :], ps, ACT.Copy).then_inc(act_drained[FRONT], 1)
                    elif kind == "qk":
                        for tensor, name in ((0, "q"), (1, "k")):
                            wait_filled(act, n, (name,))
                            if tensor == 0 and not first:
                                act.wait_ge(stacked, at(n - 1, 16 * STACK_DMAS, 16 * STACK_DMAS))
                            act.activation(qk_parts[:, tensor, 0, :], PS[0:C, bank((name,)), :], ACT.Copy
                                           ).then_inc(act_drained[FRONT], 1)
                    elif kind == "v":
                        wait_filled(act, n, step)
                        if not first:
                            wait_filled(act, n - 1, ("pv", 1))
                        act.activation(v_aug[:, :, :, 0:D],
                                       PS[:, bank(step), 0:TILES * C].rearrange("p (t h d) -> p t h d", h=HEADS, d=D),
                                       ACT.Copy).then_inc(act_drained[FRONT], 1)
                    elif kind == "shift":
                        wait_filled(act, n, step)
                        if not first:
                            act.wait_ge(shift_placed, at(n - 1, 16, 16))
                        act.activation(shift_t[:, :], PS[0:SHIFT * HEADS, bank(step), 0:PT // 2].bitcast(BF16), ACT.Copy
                                       ).then_inc(act_drained[ATTN], 1)
                    elif kind == "prob":
                        _, b, k = step
                        wait_filled(act, n, step)
                        if k == 0 and not first:
                            wait_filled(act, n - 1, ("pv", b))
                        if k < 3:
                            dst = prob_a[:, b, 2 * k:2 * k + 2, :].rearrange("p h t -> p (h t)")
                        else:
                            dst = prob_b[:, b, 4 * (k - 3):min(4 * (k - 3) + 4, HEADS), :].rearrange("p h t -> p (h t)")
                        act.activation(dst, PS[:, bank(step), 0:dst.shape[1]], ACT.Exp, scale=SCALE
                                       ).then_inc(act_drained[ATTN], 1)
                    elif kind == "pv":
                        b = step[1]
                        wait_filled(act, n, step)
                        if not first:
                            wait_filled(act, n - 1, ("out_t", b))
                        act.activation(att_t[:, b, :, :].rearrange("p g t -> p (g t)"), PS[0:C, bank(step), :], ACT.Copy
                                       ).then_inc(act_drained[ATTN], 1)
                    elif kind == "heads_t":
                        wait_filled(act, n, step)
                        act.activation(heads_t[0:C, :], PS[0:C, bank(step), :], ACT.Copy).then_inc(act_drained[ATTN], 1)
                    elif kind == "norm2_t":
                        wait_filled(act, n, step)
                        ps = PS[0:C, bank(step), :]
                        act.activation(t2_f[0:C, :], ps, ACT.Copy)
                        act.activation(t2_hi[0:C, :], ps, ACT.Copy).then_inc(act_drained[ATTN], 1)
                    elif kind == "gate2":
                        act.wait_ge(gdiff_ready, at(n, 1, 1))
                        act.activation(gexp[:, :, :], gdiff[:, :, :], ACT.Exp).then_inc(gexp_ready, 1)

            iterations(act, body)

        @block.tensor
        def _(pe):
            def split_product(dst, a_hi, a_lo, b_hi, b_lo):
                pe.matmul(dst, a_hi, b_hi, start=True, stop=False)
                pe.matmul(dst, a_hi, b_lo, start=False, stop=False)
                return pe.matmul(dst, a_lo, b_hi, start=False, stop=True)

            pe.wait_ge(const_ready, 9)
            for p in range(PAIRS):
                if p % (PAIRS // X_LOADS) == 0:
                    pe.wait_ge(x_loaded[p // (PAIRS // X_LOADS)], 16)
                for t in range(TILES):
                    last = pe.transpose(PS[0:C, p, t * P:(t + 1) * P], X[:, p * TILES + t, :], ident[:, :])
                last.then_inc(xt_filled, 1)
            pe.wait_ge(xt_copied, 1)
            pe.wait_ge(gn_step, 1)
            pe.matmul(PS[0:C, 0, 0:IMAGES], group_avg[:, :], gn_mv[:, :, 0], start=True, stop=True).then_inc(gn_averaged, 1)
            pe.wait_ge(gn_step, 5)
            pe.matmul(PS[0:C, 0, IMAGES:2 * IMAGES], group_avg[:, :], gn_spread[:, :], start=True, stop=True
                      ).then_inc(gn_averaged, 1)
            pe.sem_inc(y_filled, HIDDEN_FREE)
            pe.wait_ge(split_lo, 3)
            pe.wait_ge(pad_ready, 14)
            pe.wait_ge(xt_copied, PAIRS)

            def body(i, stages):
                for step, kind, n in steps_of(i, stages):
                    if kind == "ffn1":
                        m = step[1]
                        if m == 0:
                            wait_act(pe, n, ("norm2_t",))
                            wait_dve(pe, n, ("norm2_t",))
                        pe.wait_ge(h_ready, at(n, BLOCKS, m - 1 + H_FREE))
                        w = slice(m * P, (m + 1) * P)
                        split_product(PS[:, HIDDEN_BANKS[m % 2], :], w1_hi[:, w], w1_lo[:, w], t2_hi[:, :], t2_lo[:, :]
                                      ).then_inc(h_filled, 1)
                    elif kind == "ffn2":
                        e = step[1]
                        pe.wait_ge(h_ready, at(n, BLOCKS, CHUNKS * (e + 1) + H_FREE))
                        pe.wait_ge(y_mixed, at(n, E1 * TILES, TILES * e + Y_FREE))
                        for t in range(TILES):
                            dst = PS[:, Y_BANK, t * C:(t + 1) * C]
                            pe.matmul(dst, ones_b[:, :], b2_parts[:, e * C:(e + 1) * C], start=True, stop=False)
                            for c in range(CHUNKS):
                                m = CHUNKS * e + c
                                mm = pe.matmul(dst, hidden[:, m, t * P:(t + 1) * P], w2_f[:, m, :],
                                               start=False, stop=c == CHUNKS - 1)
                        mm.then_inc(y_filled, 1)
                    elif kind == "conv":
                        pe.wait_ge(xn_hi_ready, at(n, 1, 1))
                        pe.wait_ge(xn_lo_ready, at(n, 1, 1))
                        for t in range(TILES):
                            wait_bank_free(pe, n, ("conv", t))
                            c = slice(t * P, (t + 1) * P)
                            split_product(PS[:, bank(("conv", t)), 0:CONV_N], xn_hi[:, c], xn_lo[:, c],
                                          conv_hi[:, :], conv_lo[:, :]).then_inc(filled[FRONT], 1)
                    elif kind in ("norm1_t", "norm2_t"):
                        which = int(kind == "norm2_t")
                        wait_bank_free(pe, n, step)
                        pe.wait_ge(normed_ready[which], at(n, TILES, TILES))
                        for t in range(TILES):
                            mm = pe.transpose(PS[0:C, bank(step), t * P:(t + 1) * P], normed[:, which, t, :], ident[:, :])
                        mm.then_inc(filled[(FRONT, ATTN)[which]], 1)
                    elif kind == "qk":
                        wait_act(pe, n, ("norm1_t",))
                        wait_dve(pe, n, ("norm1_t",))
                        for tensor, name in ((0, "q"), (1, "k")):
                            wait_bank_free(pe, n, (name,))
                            split_product(PS[0:C, bank((name,)), :], qk_hi[:, tensor, :], qk_lo[:, tensor, :],
                                          t1_hi[:, :], t1_lo[:, :]).then_inc(filled[FRONT], 1)
                    elif kind == "v":
                        wait_bank_free(pe, n, step)
                        for t in range(TILES):
                            mm = pe.matmul(PS[:, bank(step), t * C:(t + 1) * C], t1_f[:, t * P:(t + 1) * P],
                                           wv_f[:, :, :].rearrange("c h d -> c (h d)"), start=True, stop=True)
                        mm.then_inc(filled[FRONT], 1)
                    elif kind == "score":
                        _, b, k = step
                        if (b, k) == (0, 0):
                            pe.wait_ge(stacked, at(n, 16 * STACK_DMAS, 16 * STACK_DMAS))
                        wait_bank_free(pe, n, step)
                        dst = PS[:, bank(step), :]
                        t0 = b * TOKENS
                        if k < 2:
                            heads = range(4 * k, min(4 * k + 4, HEADS))
                            width = len(heads)
                            pe.matmul(dst[:, 0:width * P], ident_b[:, :],
                                      causal_b[:, :].unsqueeze(1).to_broadcast([P, width, P]), start=True, stop=False,
                                      skip_group_check=True)
                            for j, h in enumerate(heads):
                                mm = pe.matmul(dst[:, j * P:(j + 1) * P], k_stack[0:STACK, h, t0:t0 + P],
                                               q_stack[0:STACK, h, t0:t0 + P], start=False, stop=j == width - 1,
                                               skip_group_check=True)
                        else:
                            heads = range(2 * (k - 2), 2 * (k - 2) + 2)
                            pe.matmul(dst.rearrange("p (h s) -> p h s", h=2)[:, :, P:TOKENS], ident_b[:, :],
                                      causal_b[:, :].unsqueeze(1).to_broadcast([P, 2, P]), start=True, stop=False,
                                      skip_group_check=True)
                            for j, h in enumerate(heads):
                                mm = pe.matmul(dst[:, j * TOKENS:(j + 1) * TOKENS], k_stack[0:STACK, h, t0 + P:t0 + TOKENS],
                                               q_stack[0:STACK, h, t0:t0 + TOKENS], start=False, stop=j == 1,
                                               skip_group_check=True)
                        mm.then_inc(filled[ATTN], 1)
                    elif kind == "shift":
                        wait_bank_free(pe, n, step)
                        pe.wait_ge(shift_ready, at(n, 1, 1))
                        for t in range(TILES):
                            mm = pe.transpose(PS[0:SHIFT * HEADS, bank(step), t * P // 2:(t + 1) * P // 2].bitcast(BF16),
                                              shift_parts[:, t, :, :].rearrange("p a h -> p (a h)"), ident_b[:, :])
                        mm.then_inc(filled[ATTN], 1)
                    elif kind == "prob":
                        _, b, k = step
                        if (b, k) == (0, 0):
                            pe.wait_ge(shift_placed, at(n, 16, 16))
                        wait_bank_free(pe, n, step)
                        dst = PS[:, bank(step), :]
                        t0 = b * TOKENS
                        if k < 3:
                            for j in range(2):
                                mm = pe.matmul(dst[:, j * TOKENS:(j + 1) * TOKENS], q_stack[:, 2 * k + j, t0:t0 + P],
                                               k_stack[:, 2 * k + j, t0:t0 + TOKENS], start=True, stop=True)
                        else:
                            for j, h in enumerate(range(4 * (k - 3), min(4 * (k - 3) + 4, HEADS))):
                                mm = pe.matmul(dst[:, j * P:(j + 1) * P], q_stack[:, h, t0 + P:t0 + TOKENS],
                                               k_stack[:, h, t0 + P:t0 + TOKENS], start=True, stop=True)
                        mm.then_inc(filled[ATTN], 1)
                    elif kind == "pv":
                        b = step[1]
                        wait_bank_free(pe, n, step)
                        pe.wait_ge(prob_ready, at(n, 4 * UNFUSED, (2 * b + 2) * UNFUSED))
                        wait_act(pe, n, ("v",))
                        for g in range(2):
                            for half in range(2):
                                for j in range(HG):
                                    h = HG * g + j
                                    probs = prob_a[:, b, h, :] if half == 0 else prob_b[:, b, h, :]
                                    first_t = g * TOKENS + half * P
                                    mm = pe.matmul(PS[HS * j:HS * (j + 1), bank(step), first_t:(g + 1) * TOKENS],
                                                   v_aug[:, 2 * b + half, h, :], probs, start=half == 0, stop=half == 1,
                                                   skip_group_check=True)
                        mm.then_inc(filled[ATTN], 1)
                    elif kind == "out_t":
                        b = step[1]
                        wait_bank_free(pe, n, step)
                        wait_act(pe, n, ("pv", b))
                        for t in range(2):
                            for g in range(2):
                                block_ = slice((2 * t + g) * C, (2 * t + g + 1) * C)
                                mm = pe.transpose(PS[:, bank(step), block_],
                                                  att_t[:, b, g, t * P:(t + 1) * P], ident[0:C, 0:C])
                        mm.then_inc(filled[ATTN], 1)
                    elif kind == "heads_t":
                        wait_bank_free(pe, n, step)
                        wait_dve(pe, n, ("out_t", 1))
                        for t in range(TILES):
                            mm = pe.transpose(PS[0:C, bank(step), t * P:(t + 1) * P], att[:, t, :], ident[:, :])
                        mm.then_inc(filled[ATTN], 1)
                    elif kind in ("proj", "gate2"):
                        lhs, rhs, source = (heads_t, wproj_f, "heads_t") if kind == "proj" else (t2_f, gate_f, "norm2_t")
                        wait_bank_free(pe, n, step)
                        wait_act(pe, n, (source,))
                        for t in range(TILES):
                            mm = pe.matmul(PS[:, bank(step), t * C:(t + 1) * C], lhs[:, t * P:(t + 1) * P], rhs[:, :],
                                           start=True, stop=True)
                        mm.then_inc(filled[ATTN], 1)
                if FFN not in stages:
                    pe.wait_ge(split_lo, 7)

            iterations(pe, body)

        @block.vector
        def _(dve):
            dve.memset(b2_f[:, :], 0.0).then_inc(pad_ready, 1)
            dve.memset(conv_f[:, CONV_N - 1:CONV_N], 0.0).then_inc(pad_ready, 1)
            dve.memset(conv_f[C:C + 1, E0 * C:CONV_N - 1], 0.0).then_inc(pad_ready, 1)
            dve.memset(gate_f[:, E1:C], 0.0).then_inc(pad_ready, 1)
            dve.memset(xn_hi[C:C + 1, :].bitcast(F32), 1.0).then_inc(pad_ready, 1)
            dve.memset(xn_lo[C:C + 1, :].bitcast(F32), 0.0).then_inc(pad_ready, 1)
            dve.memset(t2_hi[C:C + 1, :].bitcast(F32), 1.0).then_inc(pad_ready, 1)
            dve.memset(t2_lo[C:C + 1, :].bitcast(F32), 0.0).then_inc(pad_ready, 1)
            dve.memset(t2_f[C:C + 1, :], 1.0).then_inc(pad_ready, 1)
            dve.memset(heads_t[C:C + 1, :], 1.0).then_inc(pad_ready, 1)
            dve.memset(q_stack[STACK:STACK + SHIFT, :, :], 1.0).then_inc(pad_ready, 1)
            dve.memset(v_aug[:, :, :, D:D + 1], 1.0).then_inc(pad_ready, 1)
            dve.memset(v_aug[:, :, :, D + 1:HS], 0.0).then_inc(pad_ready, 1)
            dve.memset(b2_parts[:, :], 0.0).then_inc(pad_ready, 1)
            dve.sem_inc(y_mixed, Y_FREE)

            for n in range(IMAGES):
                dve.wait_ge(xt_copied, n // 2 + 1)
                dve.bn_stats(gn_stats[:, n, :], XT[:, n * TOKENS:(n + 1) * TOKENS]).then_inc(gn_stat, 1)
            for n in range(IMAGES):
                dve.wait_ge(gn_stat, n + 1)
                last = dve.bn_aggr(gn_mv[:, n, :], gn_stats[:, n, :])
            last.then_inc(gn_step, 1)
            dve.wait_ge(gn_averaged, 1)
            dve.tensor_copy(gn_mean[:, :], PS[0:C, 0, 0:IMAGES]).then_inc(gn_step, 1)
            dve.wait_ge(gn_step, 2)
            dve.tensor_tensor(gn_dev[:, :], gn_mv[:, :, 0], gn_mean[:, :], ALU.subtract).then_inc(gn_step, 1)
            dve.wait_ge(gn_step, 3)
            dve.tensor_tensor(gn_square[:, :], gn_dev[:, :], gn_dev[:, :], ALU.mult).then_inc(gn_step, 1)
            dve.wait_ge(gn_step, 4)
            dve.tensor_tensor(gn_spread[:, :], gn_square[:, :], gn_mv[:, :, 1], ALU.add).then_inc(gn_step, 1)
            dve.wait_ge(gn_averaged, 2)
            dve.tensor_copy(gn_var[:, :], PS[0:C, 0, IMAGES:2 * IMAGES]).then_inc(gn_step, 1)
            dve.wait_ge(split_hi, 1)
            dve.tensor_tensor(conv_lo[:, :], conv_f[:, :], conv_hi[:, :].bitcast(F32), ALU.subtract).then_inc(split_lo, 1)
            dve.wait_ge(split_hi, 3)
            for tensor in range(2):
                dve.tensor_tensor(qk_lo[:, tensor, :].rearrange("c (d h) -> c d h", h=HEADS),
                                  qk_f[:, tensor, :, :].rearrange("c h d -> c d h"),
                                  qk_hi[:, tensor, :].rearrange("c (d h) -> c d h", h=HEADS).bitcast(F32),
                                  ALU.subtract).then_inc(split_lo, 1)

            def normalise_x(i):
                if not is_first(i):
                    dve.wait_ge(xn_hi_ready, at(i - 1, 1, 1))
                    dve.wait_ge(xn_lo_ready, at(i - 1, 1, 1))
                for b in range(2):
                    n = i * 2 + b
                    dve.tensor_scalar(xn[:, b * TOKENS:(b + 1) * TOKENS], XT[:, bass.ds(n * TOKENS, TOKENS)],
                                      gn_mean[:, bass.ds(n, 1)], gn_scale[:, bass.ds(n, 1)],
                                      ALU.subtract, ALU.mult).then_inc(xn_ready, 1)

            dve.wait_ge(gn_root, 2)
            dve.wait_ge(split_hi, 4)
            dve.tensor_tensor(w1_lo[:, :], w1_f[:, :, :].rearrange("c e h -> c (e h)"), w1_hi[:, :].bitcast(F32),
                              ALU.subtract).then_inc(split_lo, 1)
            dve.tensor_copy(b2_lead[:, 0, :], b2_f[:, :]).then_inc(b2_step, 1)
            dve.wait_ge(b2_step, 1)
            dve.tensor_tensor(b2_rest[:, 0, :], b2_f[:, :], b2_lead[:, 0, :], ALU.subtract).then_inc(b2_step, 1)
            dve.wait_ge(b2_step, 2)
            dve.tensor_copy(b2_lead[:, 1, :], b2_rest[:, 0, :]).then_inc(b2_step, 1)
            dve.wait_ge(b2_step, 3)
            dve.tensor_tensor(b2_rest[:, 1, :], b2_rest[:, 0, :], b2_lead[:, 1, :], ALU.subtract).then_inc(b2_step, 1)
            dve.tensor_copy(b2_parts[0:1, :], b2_lead[0:1, 0, :]).then_inc(split_lo, 1)
            dve.tensor_copy(b2_parts[32:33, :], b2_lead[32:33, 1, :]).then_inc(split_lo, 1)
            dve.wait_ge(b2_step, 4)
            dve.tensor_copy(b2_parts[64:65, :], b2_rest[64:65, 1, :]).then_inc(split_lo, 1)

            steps = {}
            stage = FRONT

            def step_done(ins):
                steps[stage] += 1
                ins.then_inc(dve_step[stage], 1)

            def wait_step(n):
                dve.wait_ge(dve_step[stage], at(n, DVE_STEPS[stage], steps[stage]))

            def top_two(n, count, value, gt, eq, before, rank, chosen):
                shape = [P, TILES, count, count]
                of_j = value.unsqueeze(2).to_broadcast(shape)
                of_e = value.unsqueeze(3).to_broadcast(shape)
                step_done(dve.tensor_tensor(gt[:, :, :, :], of_j, of_e, ALU.is_gt))
                step_done(dve.tensor_tensor(eq[:, :, :, :], of_j, of_e, ALU.is_equal))
                wait_step(n)
                step_done(dve.tensor_tensor(eq[:, :, :, :], eq[:, :, :, :],
                                            before[:, :, :].unsqueeze(1).to_broadcast(shape), ALU.mult))
                wait_step(n)
                step_done(dve.tensor_tensor(gt[:, :, :, :], gt[:, :, :, :], eq[:, :, :, :], ALU.add))
                wait_step(n)
                step_done(dve.tensor_reduce(rank[:, :, :], gt[:, :, :, :], AX_X, ALU.add))
                wait_step(n)
                step_done(dve.tensor_scalar(chosen[:, :, :], rank[:, :, :], 1.5, None, ALU.is_lt))
                wait_step(n)

            def row_statistics(n, which, rows):
                base = steps[stage]
                for t in range(TILES):
                    step_done(dve.bn_stats(ln_stats[:, which, t, :], rows[:, t, :]))
                for t in range(TILES):
                    dve.wait_ge(dve_step[stage], at(n, DVE_STEPS[stage], base + t + 1))
                    dve.bn_aggr(ln_mv[:, which, t, :], ln_stats[:, which, t, :]).then_inc(ln_ready[which], UNFUSED)

            def normalise_rows(n, which, rows):
                if not is_first(n):
                    wait_filled(dve, n - 1, (("norm1_t",), ("norm2_t",))[which])
                dve.wait_ge(rstd_ready[which], at(n, 1, 1))
                for t in range(TILES):
                    dve.tensor_scalar(normed[:, which, t, :], rows[:, t, :], ln_mv[:, which, t, 0:1],
                                      ln_scale[:, which, t:t + 1], ALU.subtract, ALU.mult).then_inc(normed_ready[which], 1)

            def body(i, stages):
                nonlocal stage
                steps.update({g: 0 for g in STAGES})
                for step, kind, n in steps_of(i, stages):
                    stage = STAGE_OF[kind]
                    first = is_first(n)
                    if kind == "xn":
                        normalise_x(n)
                    elif kind == "norm1":
                        normalise_rows(n, 0, res1)
                    elif kind == "norm2":
                        normalise_rows(n, 1, res2)
                    elif kind == "ffn2":
                        e = step[1]
                        dve.wait_ge(y_filled, at(n, E1, e + 1 + HIDDEN_FREE))
                        if e == 0:
                            dve.wait_ge(stored, at(n, 16, STORE_FREE))
                        for t in range(TILES):
                            dve.wait_ge(y_mixed, at(n, E1 * TILES, TILES * (e - 1) + t + 1 + Y_FREE))
                            dve.scalar_tensor_tensor(
                                result[:, t, :], PS[:, Y_BANK, t * C:(t + 1) * C], weight1[:, t, e:e + 1],
                                res2[:, t, :] if e == 0 else result[:, t, :], ALU.mult, ALU.add).then_inc(y_mixed, 1)
                    elif kind == "gates":
                        wait_act(dve, n, ("conv", TILES - 1))
                        logit = conv_y[:, :, E0 * C:E0 * C + E0]
                        top_two(n, E0, logit, gt0, eq0, before0, rank0, chosen0)
                        step_done(dve.tensor_tensor(picked0[:, :, :], chosen0[:, :, :], logit, ALU.mult))
                        wait_step(n)
                        step_done(dve.tensor_reduce(sum0[:, :], picked0[:, :, :], AX_X, ALU.add))
                        wait_step(n)
                        dve.scalar_tensor_tensor(arg0[:, :, :], sum0[:, :].unsqueeze(2).to_broadcast([P, TILES, E0]), -0.5,
                                                 logit, ALU.mult, ALU.add).then_inc(arg0_ready, 1)
                        dve.wait_ge(tanh0_ready, at(n, 1, 1))
                        step_done(dve.tensor_scalar(half0[:, :, :], tanh0[:, :, :], 0.5, 0.5, ALU.mult, ALU.add))
                        wait_step(n)
                        step_done(dve.tensor_tensor(weight0[:, :, :], half0[:, :, :], chosen0[:, :, :], ALU.mult))
                        wait_step(n)
                    elif kind == "mix":
                        base = steps[stage]
                        for e in range(E0):
                            for t in range(TILES):
                                y = conv_y[:, t, e * C:(e + 1) * C]
                                if e == 0:
                                    step_done(dve.tensor_scalar(mixed[:, t, :], y, weight0[:, t, 0:1], None, ALU.mult))
                                    continue
                                dve.wait_ge(dve_step[stage], at(n, DVE_STEPS[stage], base + TILES * (e - 1) + t + 1))
                                step_done(dve.scalar_tensor_tensor(mixed[:, t, :], y, weight0[:, t, e:e + 1], mixed[:, t, :],
                                                                   ALU.mult, ALU.add))
                        wait_step(n)
                        step_done(dve.scalar_tensor_tensor(leaky[:, :, :], mixed[:, :, :], 0.01, mixed[:, :, :],
                                                           ALU.mult, ALU.max))
                        wait_step(n)
                        if not first:
                            dve.wait_ge(held_ready, at(n - 1, UNFUSED, UNFUSED))
                        dve.tensor_tensor(res1[:, :, :], leaky[:, :, :], X[:, bass.ds(n * TILES, TILES), :], ALU.add
                                          ).then_inc(res_ready, 1)
                        dve.wait_ge(res_ready, at(n, 1, 1))
                        row_statistics(n, 0, res1)
                    elif kind in ("norm1_t", "norm2_t"):
                        lo, hi = (t1_lo, t1_hi) if kind == "norm1_t" else (t2_lo, t2_hi)
                        wait_filled(dve, n, step)
                        wait_act(dve, n, step)
                        dve.tensor_tensor(lo[0:C, :], PS[0:C, bank(step), :], hi[0:C, :].bitcast(F32), ALU.subtract
                                          ).then_inc(dve_drained[stage], 1)
                    elif kind == "qk":
                        for tensor, name in ((0, "q"), (1, "k")):
                            wait_filled(dve, n, (name,))
                            wait_act(dve, n, (name,))
                            if not first:
                                dve.wait_ge(low_ready, at(n - 1, 2 * UNFUSED, (tensor + 1) * UNFUSED))
                            ins = dve.tensor_tensor(qk_rest[:, tensor, :], PS[0:C, bank((name,)), :],
                                                    qk_parts[:, tensor, 0, :], ALU.subtract)
                            ins.then_inc(dve_drained[stage], 1)
                    elif kind == "score":
                        _, b, k = step
                        wait_filled(dve, n, step)
                        ps = PS[:, bank(step), :]
                        if k < 2:
                            width = min(4, HEADS - 4 * k)
                            dst, src = row_max[:, 2 * b, 4 * k:4 * k + width], ps[:, 0:width * P].rearrange("p (h s) -> p h s", s=P)
                        else:
                            dst = row_max[:, 2 * b + 1, 2 * (k - 2):2 * (k - 2) + 2]
                            src = ps.rearrange("p (h s) -> p h s", s=TOKENS)
                        dve.tensor_reduce(dst, src, AX_X, ALU.max).then_inc(dve_drained[stage], 1)
                    elif kind == "shift":
                        wait_dve(dve, n, ("score", 1, 4))
                        if not first:
                            wait_filled(dve, n - 1, step)
                        lead = shift_parts[:, :, 0, :]
                        step_done(dve.tensor_scalar(lead, row_max[:, :, :], -1.0, None, ALU.mult))
                        wait_step(n)
                        step_done(dve.scalar_tensor_tensor(shift_rest[:, :, :], row_max[:, :, :], -1.0, lead,
                                                           ALU.mult, ALU.subtract))
                        wait_step(n)
                        step_done(dve.tensor_copy(shift_parts[:, :, 1, :], shift_rest[:, :, :]))
                        wait_step(n)
                        dve.tensor_tensor(shift_parts[:, :, 2, :], shift_rest[:, :, :], shift_parts[:, :, 1, :], ALU.subtract
                                          ).then_inc(shift_ready, 1)
                    elif kind == "out_t":
                        b = step[1]
                        wait_filled(dve, n, step)
                        rows = PS[:, bank(step), 0:4 * C].rearrange("p (n d) -> p n d", d=HS)
                        step_done(dve.reciprocal(inv_sum[:, b, :], rows[:, :, D]))
                        wait_step(n)
                        if b == 0 and not first:
                            wait_filled(dve, n - 1, ("heads_t",))
                        dve.tensor_tensor(att[:, 2 * b:2 * b + 2, :].rearrange("p t (h d) -> p (t h) d", d=D),
                                          rows[:, :, 0:D], inv_sum[:, b, :].unsqueeze(2).to_broadcast([P, 4 * HG, D]),
                                          ALU.mult).then_inc(dve_drained[stage], 1)
                    elif kind == "proj":
                        wait_filled(dve, n, step)
                        dve.wait_ge(held_ready, at(n, UNFUSED, UNFUSED))
                        if FFN in stages:
                            dve.wait_ge(y_mixed, at(n - 1, E1 * TILES, TILES + Y_FREE))
                        dve.tensor_tensor(res2[:, :, :].rearrange("p t c -> p (t c)"), PS[:, bank(step), 0:TILES * C],
                                          held[:, :, :].rearrange("p t c -> p (t c)"), ALU.add).then_inc(dve_drained[stage], 1)
                        wait_dve(dve, n, step)
                        row_statistics(n, 1, res2)
                    elif kind == "gate2":
                        wait_filled(dve, n, step)
                        ps = PS[:, bank(step), 0:TILES * C].rearrange("p (t c) -> p t c", c=C)[:, :, 0:E1]
                        dve.tensor_copy(glogit[:, :, :], ps).then_inc(dve_drained[stage], 1)
                        wait_dve(dve, n, step)
                        step_done(dve.tensor_reduce(gmax[:, :], glogit[:, :, :], AX_X, ALU.max))
                        wait_step(n)
                        wide = [P, TILES, E1]
                        dve.tensor_tensor(gdiff[:, :, :], glogit[:, :, :], gmax[:, :].unsqueeze(2).to_broadcast(wide),
                                          ALU.subtract).then_inc(gdiff_ready, 1)
                    elif kind == "weights":
                        wide = [P, TILES, E1]
                        dve.wait_ge(gexp_ready, at(n, 1, 1))
                        step_done(dve.tensor_reduce(gsum[:, :], gexp[:, :, :], AX_X, ALU.add))
                        wait_step(n)
                        step_done(dve.reciprocal(ginv[:, :], gsum[:, :]))
                        wait_step(n)
                        step_done(dve.tensor_tensor(gprob[:, :, :], gexp[:, :, :], ginv[:, :].unsqueeze(2).to_broadcast(wide),
                                                    ALU.mult))
                        wait_step(n)
                        top_two(n, E1, gprob[:, :, :], gt1, eq1, before1, rank1, chosen1)
                        step_done(dve.tensor_tensor(gpick[:, :, :], gprob[:, :, :], chosen1[:, :, :], ALU.mult))
                        wait_step(n)
                        step_done(dve.tensor_reduce(gpsum[:, :], gpick[:, :, :], AX_X, ALU.add))
                        wait_step(n)
                        step_done(dve.tensor_scalar(gpeps[:, :], gpsum[:, :], 1e-9, None, ALU.add))
                        wait_step(n)
                        step_done(dve.reciprocal(gpinv[:, :], gpeps[:, :]))
                        wait_step(n)
                        dve.wait_ge(y_mixed, at(n, E1 * TILES, Y_FREE))
                        step_done(dve.tensor_tensor(weight1[:, :, :], gpick[:, :, :], gpinv[:, :].unsqueeze(2).to_broadcast(wide),
                                                    ALU.mult))
                        wait_step(n)
                assert all(steps[g] == DVE_STEPS[g] for g in stages), steps

            iterations(dve, body)


_INS = ["x", "L0_conv_Wg", "L0_conv_We", "L0_conv_be", "L1_attn_wk", "L1_attn_wq", "L1_attn_wv", "L1_attn_wproj",
        "L1_attn_bproj", "L1_ffn_gate_w", "L1_ffn_gate_b", "L1_ffn_w1", "L1_ffn_b1", "L1_ffn_w2", "L1_ffn_b2"]
_OUTS = [((IMAGES, 16, 16, C), "float32")]


def kernel(**inputs):
    import numpy as _np
    import concourse.bacc as _bacc
    from concourse import mybir as _mybir
    from concourse.bass_utils import run_bass_kernel_spmd as _run

    nc = _bacc.Bacc("TRN2", target_bir_lowering=False, num_devices=1)
    arrays, args = {}, []
    for name in _INS:
        a = _np.ascontiguousarray(inputs[name])
        arrays[f"in_{name}_dram"] = a
        args.append(nc.dram_tensor(f"in_{name}_dram", a.shape, _mybir.dt.from_np(a.dtype), kind="ExternalInput").ap())
    for i, (shape, dtype) in enumerate(_OUTS):
        dt = _mybir.dt.from_np(_np.dtype(dtype))
        args.append(nc.dram_tensor(f"out_{i}_dram", shape, dt, kind="ExternalOutput").ap())
    build(nc, *args)
    r = _run(nc, [arrays], core_ids=[0])
    got = tuple(r.results[0][f"out_{i}_dram"] for i in range(len(_OUTS)))
    return got[0]
```

```python
from contextlib import ExitStack

import concourse.bass as bass
from concourse import mybir

ALU = mybir.AluOpType
ACT = mybir.ActivationFunctionType
AX_X = mybir.AxisListType.X
F32 = mybir.dt.float32
F32R = mybir.dt.float32r
BF16 = mybir.dt.bfloat16

P = 128
IMAGES, TOKENS, C = 16, 256, 96
GROUPS = 32
GC = C // GROUPS
E0 = 5
E1 = 4
HEADS, D = 6, 16
HID = 384
TILES = 4
PT = TILES * P
PAIRS = IMAGES * TOKENS // PT
CHUNKS = HID // P
BLOCKS = E1 * CHUNKS
HG = 3
HS = 32
CONV_N = E0 * C + E0 + 1
SCALE = float(C) ** -0.5
MASKED = -1.0e30
K_PARTS = (0, 0, 1, 0, 2, 1)
Q_PARTS = (0, 1, 0, 2, 0, 1)
STACK = len(K_PARTS) * D
SHIFT = 3
X_LOADS = ((0, 1), (1, 2), (2, 4), (4, 6), (6, 8))

FRONT, ATTN, TAIL, FFN = STAGES = range(4)
STAGE_OF = {"xn": FRONT, "conv": FRONT, "gates": FRONT, "mix": FRONT, "stats1": FRONT, "norm1": FRONT, "norm1_t": FRONT,
            "qk": FRONT, "v": FRONT,
            "score": ATTN, "shift": ATTN, "prob": ATTN, "pv": ATTN, "out_t": ATTN,
            "heads_t": TAIL, "proj": TAIL, "norm2": TAIL, "norm2_t": TAIL, "gate2": TAIL, "weights": TAIL, "ffn1": TAIL,
            "ffn2": FFN}
PE, SCALAR, VECTOR, GPSIMD, SYNC = range(5)
ORDER = {
    PE: [
        ("heads_t",), ("ffn2", 0), ("proj",), ("ffn2", 1), ("conv",), ("score", 0, 0), ("norm2_t",),
        ("score", 0, 1), ("ffn2", 2), ("score", 0, 2), ("ffn1", 0), ("score", 0, 3), ("ffn1", 1),
        ("score", 0, 4), ("score", 1, 0), ("ffn1", 2), ("ffn1", 3), ("score", 1, 1), ("score", 1, 2),
        ("ffn1", 4), ("score", 1, 3), ("score", 1, 4), ("gate2",), ("ffn1", 5), ("ffn1", 6), ("shift",),
        ("ffn1", 7), ("ffn1", 8), ("ffn2", 3), ("prob", 0, 0), ("prob", 0, 1), ("ffn1", 9), ("prob", 0, 2),
        ("prob", 0, 3), ("ffn1", 10), ("prob", 0, 4), ("prob", 1, 0), ("prob", 1, 1), ("prob", 1, 2),
        ("prob", 1, 3), ("prob", 1, 4), ("norm1_t",), ("pv", 0), ("qk", 0), ("pv", 1), ("out_t", 0),
        ("qk", 1), ("out_t", 1), ("ffn1", 11), ("v",)],
    SCALAR: [
        ("heads_t",), ("xn",), ("conv",), ("norm2_t",), ("ffn1", 0), ("gates", 0), ("ffn1", 1), ("ffn1", 2),
        ("ffn1", 3), ("ffn1", 4), ("mix", 0), ("ffn1", 5), ("ffn1", 6), ("shift",), ("ffn1", 7), ("ffn1", 8),
        ("prob", 0, 0), ("prob", 0, 1), ("prob", 0, 2), ("prob", 0, 3), ("prob", 0, 4), ("prob", 1, 0),
        ("prob", 1, 1), ("prob", 1, 2), ("prob", 1, 3), ("prob", 1, 4), ("norm1_t",), ("ffn1", 9), ("pv", 0),
        ("qk", 0), ("pv", 1), ("gate2",), ("qk", 1), ("ffn1", 10), ("ffn1", 11), ("v",)],
    VECTOR: [
        ("ffn2", 0), ("xn",), ("proj",), ("norm2",), ("ffn2", 1), ("score", 0, 0), ("score", 0, 1),
        ("norm2_t",), ("gates", 0), ("score", 0, 2), ("score", 0, 3), ("gates", 1), ("score", 0, 4),
        ("score", 1, 0), ("ffn2", 2), ("score", 1, 1), ("score", 1, 2), ("score", 1, 3), ("score", 1, 4),
        ("shift",), ("mix", 1), ("mix", 2), ("mix", 3), ("mix", 4), ("stats1",), ("norm1",), ("norm1_t",),
        ("gate2",), ("qk", 0), ("ffn2", 3), ("out_t", 0), ("out_t", 1), ("qk", 1), ("weights",)],
    GPSIMD: [
        ("xn",), ("norm2",), ("norm1",), ("prob", 0, 2), ("prob", 0, 4), ("prob", 1, 2), ("prob", 1, 4),
        ("qk", 0), ("qk", 1)],
    SYNC: [
        ("shift",), ("qk", 0), ("qk", 1), ("ffn2", 3)]}

HIDDEN_BANKS = (0, 1)
Y_BANK = 2
RING = {FRONT: (3, 4), ATTN: (5, 6), TAIL: (7,)}
UNFUSED = 2
DRAINS = {"conv": "S", "norm1_t": "SV", "qk": "SV", "v": "S", "score": "V", "shift": "S",
          "prob": "S", "pv": "S", "out_t": "V", "heads_t": "S", "proj": "V", "norm2_t": "SV", "gate2": "V"}


def fills_of(steps):
    fills = []
    for step in steps:
        if step[0] == "conv":
            fills += [("conv", t) for t in range(TILES)]
        elif step[0] in DRAINS:
            fills.append(step)
    return fills


FILLS = {g: [f for f in fills_of(ORDER[PE]) if STAGE_OF[f[0]] == g] for g in RING}
EMPTIED = {(g, e): [f for f in fills_of(ORDER[e]) if STAGE_OF[f[0]] == g and letter in DRAINS[f[0]]]
           for g in RING for e, letter in ((SCALAR, "S"), (VECTOR, "V"))}
LAST_PROB = [f for f in FILLS[ATTN] if f[0] == "prob"][-1]
DVE_STEPS = {FRONT: 29, ATTN: 5, TAIL: 17, FFN: 0}


def at(i, per, n):
    return i * per + n


def build(nc, x, conv_gate, conv_w, conv_b, wk, wq, wv, wproj, bproj, gate_w, gate_b, w1, b1, w2, b2, out):
    x_t = x.rearrange("b h w c -> (b h w) c").rearrange("(t p) c -> p t c", p=P)
    out_t = out.rearrange("b h w c -> (b h w) c").rearrange("(t p) c -> p t c", p=P)

    with ExitStack() as ctx:
        def sb(name, shape, dt=F32):
            return ctx.enter_context(nc.sbuf_tensor(name, shape, dt))

        def sem(name):
            return ctx.enter_context(nc.semaphore(name))

        PS = ctx.enter_context(nc.psum_tensor("PS", [P, 8, 512], F32))

        ones = sb("ones", [P, P])
        ident = sb("ident", [P, P])
        ident_b = sb("ident_b", [P, P], BF16)
        zeros_b = sb("zeros_b", [P, P], BF16)
        causal_b = sb("causal_b", [P, P], BF16)
        group_avg = sb("group_avg", [C, C])
        ones_b = sb("ones_b", [P, P], BF16)
        before0 = sb("before0", [P, E0, E0])
        before1 = sb("before1", [P, E1, E1])
        eps_t = sb("eps_t", [P, 32])
        power_t = sb("power_t", [P, 32])
        conv_f = sb("conv_f", [C + 1, CONV_N])
        conv_hi = sb("conv_hi", [P, CONV_N], F32R)
        conv_lo = sb("conv_lo", [P, CONV_N], F32R)
        qk_f = sb("qk_f", [C, 2, HEADS, D])
        qk_hi = sb("qk_hi", [C, 2, C], F32R)
        qk_lo = sb("qk_lo", [C, 2, C], F32R)
        wv_f = sb("wv_f", [C, HEADS, D])
        wv_hi = sb("wv_hi", [C, C], F32R)
        wv_lo = sb("wv_lo", [C, C], F32R)
        wproj_f = sb("wproj_f", [P, C])
        gate_f = sb("gate_f", [P, C])
        gate_both = sb("gate_both", [P, C], F32R)
        gate_hi = sb("gate_hi", [P, C], F32R)
        w1_f = sb("w1_f", [C + 1, E1, HID])
        w1_hi = sb("w1_hi", [P, E1 * HID], F32R)
        w1_lo = sb("w1_lo", [P, E1 * HID], F32R)
        w2_f = sb("w2_f", [P, BLOCKS, C])
        b2_f = sb("b2_f", [65, E1 * C])
        b2_lead = sb("b2_lead", [65, 2, E1 * C], BF16)
        b2_rest = sb("b2_rest", [65, 2, E1 * C])
        b2_parts = sb("b2_parts", [P, E1 * C], BF16)
        X = sb("X", [P, IMAGES * TOKENS // P, C])
        XT = sb("XT", [C, IMAGES * TOKENS])
        gn_stats = sb("gn_stats", [C, IMAGES, 6])
        gn_mv = sb("gn_mv", [C, IMAGES, 2])
        gn_mean = sb("gn_mean", [C, IMAGES])
        gn_var = sb("gn_var", [C, IMAGES])
        gn_dev = sb("gn_dev", [C, IMAGES])
        gn_scale = sb("gn_scale", [C, IMAGES])
        gn_square = sb("gn_square", [C, IMAGES])
        gn_spread = sb("gn_spread", [C, IMAGES])
        gn_veps = sb("gn_veps", [C, IMAGES])
        xn = sb("xn", [C, PT])
        xn_hi = sb("xn_hi", [P, PT], F32R)
        xn_lo = sb("xn_lo", [P, PT], F32R)
        conv_y = sb("conv_y", [P, TILES, CONV_N])
        beats0 = sb("beats0", [P, TILES, E0, 2 * E0])
        rank0 = sb("rank0", [P, TILES, E0])
        chosen0 = sb("chosen0", [P, TILES, E0])
        picked0 = sb("picked0", [P, TILES, E0])
        sum0 = sb("sum0", [P, TILES])
        arg0 = sb("arg0", [P, TILES, E0])
        tanh0 = sb("tanh0", [P, TILES, E0])
        half0 = sb("half0", [P, TILES, E0])
        weight0 = sb("weight0", [P, TILES, E0])
        mixed = sb("mixed", [P, TILES, C])
        leaky = sb("leaky", [P, TILES, C])
        res1s = [sb(f"res1_{n}", [P, TILES, C]) for n in range(2)]
        res2 = sb("res2", [P, TILES, C])
        ln_stats = sb("ln_stats", [P, 2, TILES, 6])
        ln_mv = sb("ln_mv", [P, 2, TILES, 2])
        ln_var = sb("ln_var", [P, 2, TILES])
        ln_scale = sb("ln_scale", [P, 2, TILES])
        normed = sb("normed", [P, 2, TILES, C])
        t1_hi = sb("t1_hi", [C, PT], F32R)
        t1_lo = sb("t1_lo", [C, PT], F32R)
        qk_parts = sb("qk_parts", [C, 2, 3, PT], BF16)
        qk_rest = sb("qk_rest", [C, 2, PT])
        q_stacks = [sb(f"q_stack{n}", [P, HEADS, PT], BF16) for n in range(2)]
        k_stacks = [sb(f"k_stack{n}", [P, HEADS, PT], BF16) for n in range(2)]
        v_augs = [sb(f"v_aug{n}", [P, TILES, HEADS, HS]) for n in range(2)]
        row_max = sb("row_max", [P, TILES, HEADS])
        shift_parts = sb("shift_parts", [P, TILES, SHIFT, HEADS], BF16)
        shift_rest = sb("shift_rest", [P, TILES, HEADS])
        shift_t = sb("shift_t", [SHIFT * HEADS, PT], BF16)
        prob_a = sb("prob_a", [P, 2, HEADS, TOKENS])
        prob_b = sb("prob_b", [P, 2, HEADS, P])
        att_t = sb("att_t", [C, 2, 2, TOKENS])
        inv_sum = sb("inv_sum", [P, 2, 4 * HG])
        att = sb("att", [P, TILES, C])
        heads_t = sb("heads_t", [P, PT])
        t2_hi = sb("t2_hi", [P, PT], F32R)
        t2_lo = sb("t2_lo", [P, PT], F32R)
        gcross = sb("gcross", [P, TILES, E1])
        glogit = sb("glogit", [P, TILES, E1])
        gmax = sb("gmax", [P, TILES])
        gdiff = sb("gdiff", [P, TILES, E1])
        gexp = sb("gexp", [P, TILES, E1])
        gsum = sb("gsum", [P, TILES])
        beats1 = sb("beats1", [P, TILES, E1, 2 * E1])
        rank1 = sb("rank1", [P, TILES, E1])
        chosen1 = sb("chosen1", [P, TILES, E1])
        gpick = sb("gpick", [P, TILES, E1])
        gpsum = sb("gpsum", [P, TILES])
        gpeps = sb("gpeps", [P, TILES])
        gpinv = sb("gpinv", [P, TILES])
        weight1 = sb("weight1", [P, TILES, E1])
        hidden = sb("hidden", [P, BLOCKS, PT])
        results = [sb(f"result{n}", [P, TILES, C]) for n in range(2)]

        x_loaded = [sem(f"x_loaded{n}") for n in range(len(X_LOADS))]
        conv_loaded = sem("conv_loaded")
        qkv_loaded = sem("qkv_loaded")
        ffn_loaded = sem("ffn_loaded")
        const_ready = sem("const_ready")
        zero_ready = sem("zero_ready")
        pad_ready = sem("pad_ready")
        late_pads = sem("late_pads")
        gn_stat = sem("gn_stat")
        b2_step = sem("b2_step")
        split_hi = sem("split_hi")
        split_lo = sem("split_lo")
        xt_filled = sem("xt_filled")
        xt_copied = sem("xt_copied")
        gn_step = sem("gn_step")
        gn_averaged = sem("gn_averaged")
        gn_root = sem("gn_root")
        names = ("front", "attn", "tail", "ffn")
        filled = {g: sem(f"filled_{names[g]}") for g in RING}
        act_drained = {g: sem(f"act_drained_{names[g]}") for g in RING}
        dve_drained = {g: sem(f"dve_drained_{names[g]}") for g in RING}
        dve_step = {g: sem(f"dve_step_{names[g]}") for g in STAGES}
        ln_step = [sem(f"ln_step{n}") for n in range(2)]
        ln_ready = [sem(f"ln_ready{n}") for n in range(2)]
        rstd_ready = [sem(f"rstd_ready{n}") for n in range(2)]
        normed_ready = [sem(f"normed_ready{n}") for n in range(2)]
        res_ready = sem("res_ready")
        xn_ready = sem("xn_ready")
        xn_hi_ready = sem("xn_hi_ready")
        xn_lo_ready = sem("xn_lo_ready")
        arg0_ready = sem("arg0_ready")
        tanh0_ready = sem("tanh0_ready")
        weight0_ready = sem("weight0_ready")
        mix_begun = sem("mix_begun")
        mid_ready = sem("mid_ready")
        low_ready = sem("low_ready")
        stacked = sem("stacked")
        shift_ready = sem("shift_ready")
        shift_placed = sem("shift_placed")
        prob_ready = sem("prob_ready")
        gdiff_ready = sem("gdiff_ready")
        gexp_ready = sem("gexp_ready")
        h_filled = sem("h_filled")
        h_ready = sem("h_ready")
        y_filled = sem("y_filled")
        y_mixed = sem("y_mixed")
        stored = [sem(f"stored{n}") for n in range(2)]

        CONV_PADS, PADS, LATE_PADS = 6, 14, 7
        FFN_LOADS = 10
        GN_BATCHES = (slice(0, 2), slice(2, IMAGES))
        STACK_DMAS = 2 * len(K_PARTS)
        H_FREE, Y_FREE, STORE_FREE, HIDDEN_FREE = 2, TILES, 16, E1

        def bank(fill):
            g = STAGE_OF[fill[0]]
            return RING[g][FILLS[g].index(fill) % len(RING[g])]

        def wait_filled(eng, n, fill):
            g = STAGE_OF[fill[0]]
            eng.wait_ge(filled[g], at(n, len(FILLS[g]), FILLS[g].index(fill) + 1))

        def wait_act(eng, n, fill):
            g = STAGE_OF[fill[0]]
            order = EMPTIED[g, SCALAR]
            eng.wait_ge(act_drained[g], at(n, len(order), order.index(fill) + 1))

        def wait_dve(eng, n, fill):
            g = STAGE_OF[fill[0]]
            order = EMPTIED[g, VECTOR]
            eng.wait_ge(dve_drained[g], at(n, len(order), order.index(fill) + 1))

        def is_first(n):
            return isinstance(n, int) and n == 0

        def wait_bank_free(pe, n, fill):
            fills = FILLS[STAGE_OF[fill[0]]]
            k = fills.index(fill)
            same = [m for m in range(len(fills)) if bank(fills[m]) == bank(fill)]
            before = [m for m in same if m < k]
            if not before:
                if is_first(n):
                    return
                before, n = same, n - 1
            last = fills[before[-1]]
            if "S" in DRAINS[last[0]]:
                wait_act(pe, n, last)
            if "V" in DRAINS[last[0]]:
                wait_dve(pe, n, last)

        def iterations(eng, body, before_second=None):
            body(0, (FRONT,), 0)
            if before_second:
                before_second()
            body(1, (FRONT, ATTN), 1)
            body(2, (FRONT, ATTN, TAIL), 0)
            body(3, STAGES, 1)
            with eng.Fori(4, PAIRS - 1, 2) as i:
                body(i, STAGES, 0)
                body(i + 1, STAGES, 1)
            body(PAIRS, (ATTN, TAIL, FFN), 0)
            body(PAIRS + 1, (TAIL, FFN), 1)
            body(PAIRS + 2, (FFN,), 0)

        def steps_of(engine, i, stages, parity):
            for step in ORDER[engine]:
                stage = STAGE_OF[step[0]]
                if stage in stages:
                    yield step, step[0], i - stage if stage else i, (parity - stage) % 2

        block = ctx.enter_context(nc.Block())

        @block.sync
        def _(sp):
            conv_loads = [(conv_f[0:C, 0:E0 * C].rearrange("c (e d) -> c e d", d=C), conv_w.rearrange("e c d -> c e d")),
                          (conv_f[0:C, E0 * C:E0 * C + E0], conv_gate),
                          (conv_f[C:C + 1, 0:E0 * C], conv_b.rearrange("(a e) d -> a (e d)", a=1))]
            qkv_loads = [(qk_f[:, 0, :, :], wq.rearrange("h c d -> c h d")),
                         (qk_f[:, 1, :, :], wk.rearrange("h c d -> c h d")),
                         (wv_f[:, :, :], wv.rearrange("h c d -> c h d"))]
            ffn_loads = [(wproj_f[0:C, :], wproj),
                         (wproj_f[C:C + 1, :], bproj.rearrange("(a n) -> a n", a=1)),
                         (gate_f[0:C, 0:E1], gate_w),
                         (gate_f[C:C + 1, 0:E1], gate_b.rearrange("(a n) -> a n", a=1)),
                         (w1_f[0:C, :, :], w1.rearrange("e c h -> c e h")),
                         (w1_f[C:C + 1, :, :], b1.rearrange("(a e) h -> a e h", a=1)),
                         (w2_f[:, :, :], w2.rearrange("e (k p) c -> p (e k) c", p=P))]
            ffn_loads += [(b2_f[r:r + 1, :], b2.rearrange("(a e) c -> a (e c)", a=1)) for r in (0, 32, 64)]
            assert len(ffn_loads) == FFN_LOADS
            for n, (p0, p1) in enumerate(X_LOADS):
                tiles = slice(p0 * TILES, p1 * TILES)
                sp.dma_start(X[:, tiles, :], x_t[:, tiles, :]).then_inc(x_loaded[n], 16)
                if n == 0:
                    for dst, src in conv_loads:
                        sp.dma_start(dst, src).then_inc(conv_loaded, 16)
            for dst, src in qkv_loads:
                sp.dma_start(dst, src).then_inc(qkv_loaded, 16)
            sp.wait_ge(pad_ready, PADS)
            for dst, src in ffn_loads:
                sp.dma_start(dst, src).then_inc(ffn_loaded, 16)

            def body(i, stages, parity):
                for step, kind, n, odd in steps_of(SYNC, i, stages, parity):
                    if kind == "qk":
                        tensor = step[1]
                        stack, parts = ((q_stacks[odd], Q_PARTS), (k_stacks[odd], K_PARTS))[tensor]
                        if tensor == 0 and not (isinstance(n, int) and n < 2):
                            wait_filled(sp, n - 2, LAST_PROB)
                        sp.wait_ge(low_ready, at(n, 2 * UNFUSED, (tensor + 1) * UNFUSED))
                        for r, part in enumerate(parts):
                            sp.dma_start(stack[r * D:(r + 1) * D, :, :], qk_parts[:, tensor, part, :]
                                         ).then_inc(stacked, 16)
                    elif kind == "shift":
                        wait_act(sp, n, step)
                        sp.dma_start(k_stacks[odd][STACK:STACK + SHIFT, :, :],
                                     shift_t[:, :]).then_inc(shift_placed, 16)
                    elif kind == "ffn2":
                        sp.wait_ge(y_mixed, at(n, E1 * TILES, E1 * TILES + Y_FREE))
                        sp.dma_start(out_t[:, bass.ds(n * TILES, TILES), :], results[odd][:, :, :]).then_inc(stored[odd], 16)

            for n in range(2):
                sp.sem_inc(stored[n], STORE_FREE)
            iterations(sp, body)
            for n in range(2):
                sp.wait_ge(stored[n], PAIRS // 2 * 16 + STORE_FREE)

        @block.gpsimd
        def _(pool):
            pool.memset(ones[:, :], 1.0).then_inc(zero_ready, 1)
            pool.memset(ident_b[:, :], 0.0).then_inc(zero_ready, 1)
            pool.memset(zeros_b[:, :], 0.0).then_inc(zero_ready, 1)
            pool.memset(group_avg[:, :], 1.0 / GC).then_inc(zero_ready, 1)
            pool.memset(ones_b[:, :], 1.0).then_inc(const_ready, 1)
            pool.memset(eps_t[:, :], 1e-5).then_inc(const_ready, 1)
            pool.memset(power_t[:, :], -0.5).then_inc(const_ready, 1)
            pool.wait_ge(zero_ready, 4)
            pool.affine_select(out=ident[:, :], in_=ones[:, :], compare_op=ALU.is_equal, fill=0.0, base=0,
                               pattern=[[-1, P]], channel_multiplier=1).then_inc(const_ready, 1)
            pool.affine_select(out=ident_b[:, :], in_=ident_b[:, :], compare_op=ALU.not_equal, fill=1.0, base=0,
                               pattern=[[-1, P]], channel_multiplier=1).then_inc(const_ready, 1)
            pool.affine_select(out=causal_b[:, :], in_=zeros_b[:, :], compare_op=ALU.is_ge, fill=MASKED, base=0,
                               pattern=[[-1, P]], channel_multiplier=1).then_inc(const_ready, 1)
            for before, n in ((before0, E0), (before1, E1)):
                pool.affine_select(out=before[:, :, :], in_=ones[:, 0:n * n].rearrange("p (e j) -> p e j", j=n),
                                   compare_op=ALU.is_gt, fill=0.0, base=0, pattern=[[1, n], [-1, n]],
                                   channel_multiplier=0).then_inc(const_ready, 1)
            g = group_avg[:, :].rearrange("p (g j) -> p g j", j=GC)
            pool.affine_select(out=g, in_=g, compare_op=ALU.is_ge, fill=0.0, base=0,
                               pattern=[[-GC, GROUPS], [0, GC]], channel_multiplier=1).then_inc(zero_ready, 1)
            pool.wait_ge(zero_ready, 5)
            pool.affine_select(out=g, in_=g, compare_op=ALU.is_ge, fill=0.0, base=GC - 1,
                               pattern=[[GC, GROUPS], [0, GC]], channel_multiplier=-1).then_inc(const_ready, 1)
            def gn_inverse_root(batch):
                cols = GN_BATCHES[batch]
                pool.wait_ge(gn_step, 6 * (batch + 1))
                pool.tensor_tensor(gn_veps[:, cols], gn_var[:, cols], eps_t[0:C, cols], ALU.add).then_inc(gn_root, 1)
                pool.wait_ge(gn_root, 2 * batch + 1)
                pool.tensor_tensor(gn_scale[:, cols], gn_veps[:, cols], power_t[0:C, cols], ALU.pow).then_inc(gn_root, 1)

            pool.wait_ge(const_ready, 9)
            rows = slice(C, P)
            late_pads_of = [(w1_hi[rows, :].bitcast(F32), 0.0), (w1_lo[rows, :].bitcast(F32), 0.0),
                            (q_stacks[0][rows, :, :], 1.0), (q_stacks[1][rows, :, :], 1.0), (heads_t[rows, :], 1.0),
                            (t2_hi[rows, :].bitcast(F32), 1.0), (t2_lo[rows, :].bitcast(F32), 0.0)]
            assert len(late_pads_of) == LATE_PADS
            for pad in late_pads_of[:3]:
                pool.memset(pad[0], pad[1]).then_inc(late_pads, 1)
            pool.wait_ge(late_pads, 3)
            gn_inverse_root(0)
            def xn_rest(n):
                pool.wait_ge(xn_ready, at(n, 2, 2))
                pool.wait_ge(xn_hi_ready, at(n, 1, 1))
                if not is_first(n):
                    wait_filled(pool, n - 1, ("conv", TILES - 1))
                pool.tensor_tensor(xn_lo[0:C, :], xn[:, :], xn_hi[0:C, :].bitcast(F32), ALU.subtract
                                   ).then_inc(xn_lo_ready, 1)

            xn_rest(0)
            gn_inverse_root(1)

            for pad in late_pads_of[3:]:
                pool.memset(pad[0], pad[1]).then_inc(late_pads, 1)
            pool.wait_ge(late_pads, LATE_PADS)

            def inverse_root(n, which):
                pool.wait_ge(ln_ready[which], at(n, TILES * UNFUSED, TILES * UNFUSED))
                pool.tensor_tensor(ln_var[:, which, :], ln_mv[:, which, :, 1], eps_t[:, 0:TILES], ALU.add
                                   ).then_inc(ln_step[which], 1)
                pool.wait_ge(ln_step[which], at(n, 1, 1))
                pool.tensor_tensor(ln_scale[:, which, :], ln_var[:, which, :], power_t[:, 0:TILES], ALU.pow
                                   ).then_inc(rstd_ready[which], 1)

            def body(i, stages, parity):
                for step, kind, n, odd in steps_of(GPSIMD, i, stages, parity):
                    if kind == "norm1":
                        inverse_root(n, 0)
                    elif kind == "norm2":
                        inverse_root(n, 1)
                    elif kind == "xn":
                        if not is_first(n):
                            xn_rest(n)
                    elif kind == "qk":
                        tensor = step[1]
                        wait_dve(pool, n, step)
                        if tensor == 0 and not is_first(n):
                            pool.wait_ge(stacked, at(n - 1, 16 * STACK_DMAS, 16 * STACK_DMAS))
                        pool.tensor_scalar(qk_parts[:, tensor, 1, :], qk_rest[:, tensor, :], 1.0, 0.0,
                                           ALU.mult, ALU.add).then_inc(mid_ready, UNFUSED)
                        pool.wait_ge(mid_ready, at(n, 2 * UNFUSED, (tensor + 1) * UNFUSED))
                        pool.tensor_tensor(qk_parts[:, tensor, 2, :], qk_rest[:, tensor, :],
                                           qk_parts[:, tensor, 1, :], ALU.subtract).then_inc(low_ready, UNFUSED)
                    elif kind == "prob":
                        b = step[1]
                        wait_act(pool, n, step)
                        block_ = prob_a[:, b, :, 0:P] if step[2] == 2 else prob_b[:, b, :, :]
                        pool.affine_select(out=block_, in_=block_, compare_op=ALU.is_ge, fill=0.0, base=0,
                                           pattern=[[0, HEADS], [1, P]], channel_multiplier=-1
                                           ).then_inc(prob_ready, UNFUSED)

            iterations(pool, body)

        @block.scalar
        def _(act):
            def xn_lead(n):
                act.wait_ge(xn_ready, at(n, 2, 2))
                if not is_first(n):
                    wait_filled(act, n - 1, ("conv", TILES - 1))
                act.activation(xn_hi[0:C, :], xn[:, :], ACT.Copy).then_inc(xn_hi_ready, 1)

            for p in range(PAIRS):
                act.wait_ge(xt_filled, p + 1)
                act.activation(XT[:, p * PT:(p + 1) * PT], PS[0:C, p, :], ACT.Copy).then_inc(xt_copied, 1)
                if p == 0:
                    act.wait_ge(conv_loaded, 16 * 3)
                    act.wait_ge(pad_ready, CONV_PADS)
                    act.activation(conv_hi[0:C + 1, :], conv_f[:, :], ACT.Copy).then_inc(split_hi, 1)
            xn_lead(0)
            act.wait_ge(qkv_loaded, 16 * 3)
            for tensor in range(2):
                act.activation(qk_hi[:, tensor, :].rearrange("c (d h) -> c d h", h=HEADS),
                               qk_f[:, tensor, :, :].rearrange("c h d -> c d h"), ACT.Copy).then_inc(split_hi, 1)
            act.activation(wv_hi[:, :], wv_f[:, :, :].rearrange("c h d -> c (h d)"), ACT.Copy).then_inc(split_hi, 1)

            act.wait_ge(ffn_loaded, 16 * FFN_LOADS)
            act.wait_ge(late_pads, 2)
            act.activation(gate_both[:, :], gate_f[:, :], ACT.Copy)
            act.activation(gate_hi[:, :], gate_f[:, :], ACT.Copy).then_inc(split_hi, 1)
            act.activation(w1_hi[0:C + 1, :], w1_f[:, :, :].rearrange("c e h -> c (e h)"), ACT.Copy).then_inc(split_hi, 1)

            act.sem_inc(h_ready, H_FREE)

            def body(i, stages, parity):
                for step, kind, n, odd in steps_of(SCALAR, i, stages, parity):
                    first = is_first(n)
                    if kind == "ffn1":
                        m = step[1]
                        if m % CHUNKS == 0:
                            act.wait_ge(y_filled, at(n - 1, E1, m // CHUNKS + 1 + HIDDEN_FREE))
                        act.wait_ge(h_filled, at(n, BLOCKS, m + 1))
                        act.activation(hidden[:, m, :], PS[:, HIDDEN_BANKS[m % 2], :], ACT.Gelu).then_inc(h_ready, 1)
                    elif kind == "xn":
                        if not first:
                            xn_lead(n)
                    elif kind == "conv":
                        if not first:
                            act.wait_ge(res_ready, at(n - 1, 1, 1))
                        for t in range(TILES):
                            wait_filled(act, n, ("conv", t))
                            act.activation(conv_y[:, t, :], PS[:, bank(("conv", t)), 0:CONV_N], ACT.Copy
                                           ).then_inc(act_drained[FRONT], 1)
                    elif kind == "gates":
                        act.wait_ge(arg0_ready, at(n, 1, 1))
                        act.activation(tanh0[:, :, :], arg0[:, :, :], ACT.Tanh).then_inc(tanh0_ready, 1)
                    elif kind == "mix":
                        act.wait_ge(weight0_ready, at(n, 1, 1))
                        for t in range(TILES):
                            act.activation(mixed[:, t, :], conv_y[:, t, 0:C], ACT.Copy, scale=weight0[:, t, 0:1]
                                           ).then_inc(mix_begun, 1)
                    elif kind == "norm1_t":
                        wait_filled(act, n, step)
                        ps = PS[0:C, bank(step), :]
                        act.activation(t1_hi[:, :], ps, ACT.Copy).then_inc(act_drained[FRONT], 1)
                    elif kind == "qk":
                        tensor = step[1]
                        wait_filled(act, n, step)
                        if tensor == 0 and not first:
                            act.wait_ge(stacked, at(n - 1, 16 * STACK_DMAS, 16 * STACK_DMAS))
                        act.activation(qk_parts[:, tensor, 0, :], PS[0:C, bank(step), :], ACT.Copy
                                       ).then_inc(act_drained[FRONT], 1)
                    elif kind == "v":
                        wait_filled(act, n, step)
                        if not (isinstance(n, int) and n < 2):
                            wait_filled(act, n - 2, ("pv", 1))
                        act.activation(v_augs[odd][:, :, :, 0:D],
                                       PS[:, bank(step), 0:TILES * C].rearrange("p (t h d) -> p t h d", h=HEADS, d=D),
                                       ACT.Copy).then_inc(act_drained[FRONT], 1)
                    elif kind == "shift":
                        wait_filled(act, n, step)
                        if not first:
                            act.wait_ge(shift_placed, at(n - 1, 16, 16))
                        act.activation(shift_t[:, :], PS[0:SHIFT * HEADS, bank(step), 0:PT // 2].bitcast(BF16), ACT.Copy
                                       ).then_inc(act_drained[ATTN], 1)
                    elif kind == "prob":
                        _, b, k = step
                        wait_filled(act, n, step)
                        if k == 0 and not first:
                            wait_filled(act, n - 1, ("pv", b))
                        if k < 3:
                            dst = prob_a[:, b, 2 * k:2 * k + 2, :].rearrange("p h t -> p (h t)")
                        else:
                            dst = prob_b[:, b, 4 * (k - 3):min(4 * (k - 3) + 4, HEADS), :].rearrange("p h t -> p (h t)")
                        act.activation(dst, PS[:, bank(step), 0:dst.shape[1]], ACT.Exp, scale=SCALE
                                       ).then_inc(act_drained[ATTN], 1)
                    elif kind == "pv":
                        b = step[1]
                        wait_filled(act, n, step)
                        if not first:
                            wait_filled(act, n - 1, ("out_t", b))
                        act.activation(att_t[:, b, :, :].rearrange("p g t -> p (g t)"), PS[0:C, bank(step), :], ACT.Copy
                                       ).then_inc(act_drained[ATTN], 1)
                    elif kind == "heads_t":
                        wait_filled(act, n, step)
                        act.activation(heads_t[0:C, :], PS[0:C, bank(step), :], ACT.Copy).then_inc(act_drained[TAIL], 1)
                    elif kind == "norm2_t":
                        wait_filled(act, n, step)
                        ps = PS[0:C, bank(step), :]
                        act.activation(t2_hi[0:C, :], ps, ACT.Copy).then_inc(act_drained[TAIL], 1)
                    elif kind == "gate2":
                        act.wait_ge(gdiff_ready, at(n, 1, 1))
                        act.activation(gexp[:, :, :], gdiff[:, :, :], ACT.Exp).then_inc(gexp_ready, 1)

            iterations(act, body)

        @block.tensor
        def _(pe):
            def split_product(dst, a_hi, a_lo, b_hi, b_lo):
                pe.matmul(dst, a_hi, b_hi, start=True, stop=False)
                pe.matmul(dst, a_hi, b_lo, start=False, stop=False)
                return pe.matmul(dst, a_lo, b_hi, start=False, stop=True)

            def group_averages(batch):
                cols = GN_BATCHES[batch]
                n = cols.stop - cols.start
                pe.wait_ge(xt_copied, batch + 1)
                pe.wait_ge(gn_step, 6 * batch + 1)
                pe.matmul(PS[0:C, batch, 0:n], group_avg[:, :], gn_mv[:, cols, 0], start=True, stop=True
                          ).then_inc(gn_averaged, 1)
                pe.wait_ge(gn_step, 6 * batch + 5)
                pe.matmul(PS[0:C, batch, n:2 * n], group_avg[:, :], gn_spread[:, cols], start=True, stop=True
                          ).then_inc(gn_averaged, 1)

            pe.wait_ge(const_ready, 9)
            for n, (p0, p1) in enumerate(X_LOADS):
                pe.wait_ge(x_loaded[n], 16)
                for p in range(p0, p1):
                    for t in range(TILES):
                        last = pe.transpose(PS[0:C, p, t * P:(t + 1) * P], X[:, p * TILES + t, :], ident[:, :])
                    last.then_inc(xt_filled, 1)
                if n == 1:
                    group_averages(0)
            group_averages(1)
            pe.sem_inc(y_filled, HIDDEN_FREE)
            pe.wait_ge(split_lo, 4)
            pe.wait_ge(pad_ready, PADS)
            pe.wait_ge(xt_copied, PAIRS)

            def prepare_rest():
                pe.wait_ge(split_lo, 9)
                pe.wait_ge(ffn_loaded, 16 * FFN_LOADS)
                pe.wait_ge(late_pads, LATE_PADS)

            def body(i, stages, parity):
                for step, kind, n, odd in steps_of(PE, i, stages, parity):
                    if kind == "ffn1":
                        m = step[1]
                        if m == 0:
                            wait_dve(pe, n, ("norm2_t",))
                        pe.wait_ge(h_ready, at(n, BLOCKS, m - 1 + H_FREE))
                        w = slice(m * P, (m + 1) * P)
                        split_product(PS[:, HIDDEN_BANKS[m % 2], :], w1_hi[:, w], w1_lo[:, w], t2_hi[:, :], t2_lo[:, :]
                                      ).then_inc(h_filled, 1)
                    elif kind == "ffn2":
                        e = step[1]
                        pe.wait_ge(h_ready, at(n, BLOCKS, CHUNKS * (e + 1) + H_FREE))
                        pe.wait_ge(y_mixed, at(n, E1 * TILES, TILES * e + Y_FREE))
                        pe.matmul(PS[:, Y_BANK, 0:TILES * C], ones_b[:, :],
                                  b2_parts[:, e * C:(e + 1) * C].unsqueeze(1).to_broadcast([P, TILES, C]),
                                  start=True, stop=False, skip_group_check=True)
                        for t in range(TILES):
                            dst = PS[:, Y_BANK, t * C:(t + 1) * C]
                            for c in range(CHUNKS):
                                m = CHUNKS * e + c
                                mm = pe.matmul(dst, hidden[:, m, t * P:(t + 1) * P], w2_f[:, m, :],
                                               start=False, stop=t == TILES - 1 and c == CHUNKS - 1,
                                               skip_group_check=True)
                        mm.then_inc(y_filled, 1)
                    elif kind == "conv":
                        pe.wait_ge(xn_hi_ready, at(n, 1, 1))
                        pe.wait_ge(xn_lo_ready, at(n, 1, 1))
                        for t in range(TILES):
                            wait_bank_free(pe, n, ("conv", t))
                            c = slice(t * P, (t + 1) * P)
                            split_product(PS[:, bank(("conv", t)), 0:CONV_N], xn_hi[:, c], xn_lo[:, c],
                                          conv_hi[:, :], conv_lo[:, :]).then_inc(filled[FRONT], 1)
                    elif kind in ("norm1_t", "norm2_t"):
                        which = int(kind == "norm2_t")
                        wait_bank_free(pe, n, step)
                        pe.wait_ge(normed_ready[which], at(n, TILES, TILES))
                        for t in range(TILES):
                            mm = pe.transpose(PS[0:C, bank(step), t * P:(t + 1) * P], normed[:, which, t, :], ident[:, :])
                        mm.then_inc(filled[STAGE_OF[kind]], 1)
                    elif kind == "qk":
                        wait_dve(pe, n, ("norm1_t",))
                        tensor = step[1]
                        wait_bank_free(pe, n, step)
                        split_product(PS[0:C, bank(step), :], qk_hi[:, tensor, :], qk_lo[:, tensor, :],
                                      t1_hi[:, :], t1_lo[:, :]).then_inc(filled[FRONT], 1)
                    elif kind == "v":
                        wait_dve(pe, n, ("norm1_t",))
                        wait_bank_free(pe, n, step)
                        for t in range(TILES):
                            rows = slice(t * P, (t + 1) * P)
                            mm = split_product(PS[:, bank(step), t * C:(t + 1) * C], t1_hi[:, rows], t1_lo[:, rows],
                                               wv_hi[:, :], wv_lo[:, :])
                        mm.then_inc(filled[FRONT], 1)
                    elif kind == "score":
                        _, b, k = step
                        if (b, k) == (0, 0):
                            pe.wait_ge(stacked, at(n, 16 * STACK_DMAS, 16 * STACK_DMAS))
                        wait_bank_free(pe, n, step)
                        dst = PS[:, bank(step), :]
                        t0 = b * TOKENS
                        if k < 2:
                            heads = range(4 * k, min(4 * k + 4, HEADS))
                            width = len(heads)
                            pe.matmul(dst[:, 0:width * P], ident_b[:, :],
                                      causal_b[:, :].unsqueeze(1).to_broadcast([P, width, P]), start=True, stop=False,
                                      skip_group_check=True)
                            for j, h in enumerate(heads):
                                mm = pe.matmul(dst[:, j * P:(j + 1) * P], k_stacks[odd][0:STACK, h, t0:t0 + P],
                                               q_stacks[odd][0:STACK, h, t0:t0 + P], start=False, stop=j == width - 1,
                                               skip_group_check=True)
                        else:
                            heads = range(2 * (k - 2), 2 * (k - 2) + 2)
                            pe.matmul(dst.rearrange("p (h s) -> p h s", h=2)[:, :, P:TOKENS], ident_b[:, :],
                                      causal_b[:, :].unsqueeze(1).to_broadcast([P, 2, P]), start=True, stop=False,
                                      skip_group_check=True)
                            for j, h in enumerate(heads):
                                mm = pe.matmul(dst[:, j * TOKENS:(j + 1) * TOKENS], k_stacks[odd][0:STACK, h, t0 + P:t0 + TOKENS],
                                               q_stacks[odd][0:STACK, h, t0:t0 + TOKENS], start=False, stop=j == 1,
                                               skip_group_check=True)
                        mm.then_inc(filled[ATTN], 1)
                    elif kind == "shift":
                        wait_bank_free(pe, n, step)
                        pe.wait_ge(shift_ready, at(n, 1, 1))
                        for t in range(TILES):
                            mm = pe.transpose(PS[0:SHIFT * HEADS, bank(step), t * P // 2:(t + 1) * P // 2].bitcast(BF16),
                                              shift_parts[:, t, :, :].rearrange("p a h -> p (a h)"), ident_b[:, :])
                        mm.then_inc(filled[ATTN], 1)
                    elif kind == "prob":
                        _, b, k = step
                        if (b, k) == (0, 0):
                            pe.wait_ge(shift_placed, at(n, 16, 16))
                        wait_bank_free(pe, n, step)
                        dst = PS[:, bank(step), :]
                        t0 = b * TOKENS
                        if k < 3:
                            for j in range(2):
                                mm = pe.matmul(dst[:, j * TOKENS:(j + 1) * TOKENS], q_stacks[odd][0:STACK + SHIFT, 2 * k + j, t0:t0 + P],
                                               k_stacks[odd][0:STACK + SHIFT, 2 * k + j, t0:t0 + TOKENS], start=True, stop=True)
                        else:
                            for j, h in enumerate(range(4 * (k - 3), min(4 * (k - 3) + 4, HEADS))):
                                mm = pe.matmul(dst[:, j * P:(j + 1) * P], q_stacks[odd][0:STACK + SHIFT, h, t0 + P:t0 + TOKENS],
                                               k_stacks[odd][0:STACK + SHIFT, h, t0 + P:t0 + TOKENS], start=True, stop=True)
                        mm.then_inc(filled[ATTN], 1)
                    elif kind == "pv":
                        b = step[1]
                        wait_bank_free(pe, n, step)
                        pe.wait_ge(prob_ready, at(n, 4 * UNFUSED, (2 * b + 2) * UNFUSED))
                        wait_act(pe, n, ("v",))
                        for g in range(2):
                            for half in range(2):
                                for j in range(HG):
                                    h = HG * g + j
                                    probs = prob_a[:, b, h, :] if half == 0 else prob_b[:, b, h, :]
                                    first_t = g * TOKENS + half * P
                                    mm = pe.matmul(PS[HS * j:HS * (j + 1), bank(step), first_t:(g + 1) * TOKENS],
                                                   v_augs[odd][:, 2 * b + half, h, :], probs, start=half == 0, stop=half == 1,
                                                   skip_group_check=True)
                        mm.then_inc(filled[ATTN], 1)
                    elif kind == "out_t":
                        b = step[1]
                        wait_bank_free(pe, n, step)
                        wait_act(pe, n, ("pv", b))
                        for t in range(2):
                            for g in range(2):
                                block_ = slice((2 * t + g) * C, (2 * t + g + 1) * C)
                                mm = pe.transpose(PS[:, bank(step), block_],
                                                  att_t[:, b, g, t * P:(t + 1) * P], ident[0:C, 0:C])
                        mm.then_inc(filled[ATTN], 1)
                    elif kind == "heads_t":
                        wait_bank_free(pe, n, step)
                        wait_dve(pe, n, ("out_t", 1))
                        for t in range(TILES):
                            mm = pe.transpose(PS[0:C, bank(step), t * P:(t + 1) * P], att[:, t, :], ident[:, :])
                        mm.then_inc(filled[TAIL], 1)
                    elif kind == "proj":
                        wait_bank_free(pe, n, step)
                        wait_act(pe, n, ("heads_t",))
                        for t in range(TILES):
                            mm = pe.matmul(PS[:, bank(step), t * C:(t + 1) * C], heads_t[:, t * P:(t + 1) * P],
                                           wproj_f[:, :], start=True, stop=True)
                        mm.then_inc(filled[TAIL], 1)
                    elif kind == "gate2":
                        wait_bank_free(pe, n, step)
                        wait_dve(pe, n, ("norm2_t",))
                        for t in range(TILES):
                            dst = PS[:, bank(step), t * C:(t + 1) * C]
                            rows = slice(t * P, (t + 1) * P)
                            pe.matmul(dst, t2_hi[:, rows], gate_both[:, :], start=True, stop=False)
                            mm = pe.matmul(dst, t2_lo[:, rows], gate_hi[:, :], start=False, stop=True)
                        mm.then_inc(filled[TAIL], 1)

            iterations(pe, body, prepare_rest)

        @block.vector
        def _(dve):
            rows = slice(C, P)
            dve.memset(conv_f[:, CONV_N - 1:CONV_N], 0.0).then_inc(pad_ready, 1)
            dve.memset(conv_f[C:C + 1, E0 * C:CONV_N - 1], 0.0).then_inc(pad_ready, 1)
            dve.memset(conv_hi[rows, :].bitcast(F32), 0.0).then_inc(pad_ready, 1)
            dve.memset(conv_lo[rows, :].bitcast(F32), 0.0).then_inc(pad_ready, 1)
            dve.memset(xn_hi[rows, :].bitcast(F32), 1.0).then_inc(pad_ready, 1)
            dve.memset(xn_lo[rows, :].bitcast(F32), 0.0).then_inc(pad_ready, 1)
            dve.memset(gate_f[:, :], 0.0).then_inc(pad_ready, 1)
            dve.memset(wproj_f[rows, :], 0.0).then_inc(pad_ready, 1)
            dve.memset(b2_f[:, :], 0.0).then_inc(pad_ready, 1)
            dve.memset(b2_parts[:, :], 0.0).then_inc(pad_ready, 1)
            for v_aug in v_augs:
                dve.memset(v_aug[:, :, :, D:D + 1], 1.0).then_inc(pad_ready, 1)
                dve.memset(v_aug[:, :, :, D + 1:HS], 0.0).then_inc(pad_ready, 1)
            dve.sem_inc(y_mixed, Y_FREE)

            def group_statistics(batch):
                cols = GN_BATCHES[batch]
                n = cols.stop - cols.start
                base = 6 * batch
                for m in range(cols.start, cols.stop):
                    dve.wait_ge(xt_copied, m // 2 + 1)
                    dve.bn_stats(gn_stats[:, m, :], XT[:, m * TOKENS:(m + 1) * TOKENS]).then_inc(gn_stat, 1)
                for m in range(cols.start, cols.stop):
                    dve.wait_ge(gn_stat, m + 1)
                    last = dve.bn_aggr(gn_mv[:, m, :], gn_stats[:, m, :])
                last.then_inc(gn_step, 1)
                dve.wait_ge(gn_averaged, 2 * batch + 1)
                dve.tensor_copy(gn_mean[:, cols], PS[0:C, batch, 0:n]).then_inc(gn_step, 1)
                dve.wait_ge(gn_step, base + 2)
                dve.tensor_tensor(gn_dev[:, cols], gn_mv[:, cols, 0], gn_mean[:, cols], ALU.subtract).then_inc(gn_step, 1)
                dve.wait_ge(gn_step, base + 3)
                dve.tensor_tensor(gn_square[:, cols], gn_dev[:, cols], gn_dev[:, cols], ALU.mult).then_inc(gn_step, 1)
                dve.wait_ge(gn_step, base + 4)
                dve.tensor_tensor(gn_spread[:, cols], gn_square[:, cols], gn_mv[:, cols, 1], ALU.add).then_inc(gn_step, 1)
                dve.wait_ge(gn_averaged, 2 * batch + 2)
                dve.tensor_copy(gn_var[:, cols], PS[0:C, batch, n:2 * n]).then_inc(gn_step, 1)

            group_statistics(0)
            def normalise_x(i):
                if not is_first(i):
                    dve.wait_ge(xn_hi_ready, at(i - 1, 1, 1))
                    dve.wait_ge(xn_lo_ready, at(i - 1, 1, 1))
                for b in range(2):
                    n = i * 2 + b
                    dve.tensor_scalar(xn[:, b * TOKENS:(b + 1) * TOKENS], XT[:, bass.ds(n * TOKENS, TOKENS)],
                                      gn_mean[:, bass.ds(n, 1)], gn_scale[:, bass.ds(n, 1)],
                                      ALU.subtract, ALU.mult).then_inc(xn_ready, 1)

            dve.wait_ge(split_hi, 1)
            dve.tensor_tensor(conv_lo[0:C + 1, :], conv_f[:, :], conv_hi[0:C + 1, :].bitcast(F32), ALU.subtract).then_inc(split_lo, 1)
            dve.wait_ge(gn_root, 2)
            normalise_x(0)
            group_statistics(1)
            dve.wait_ge(split_hi, 3)
            for tensor in range(2):
                dve.tensor_tensor(qk_lo[:, tensor, :].rearrange("c (d h) -> c d h", h=HEADS),
                                  qk_f[:, tensor, :, :].rearrange("c h d -> c d h"),
                                  qk_hi[:, tensor, :].rearrange("c (d h) -> c d h", h=HEADS).bitcast(F32),
                                  ALU.subtract).then_inc(split_lo, 1)
            dve.wait_ge(split_hi, 4)
            dve.tensor_tensor(wv_lo[:, :], wv_f[:, :, :].rearrange("c h d -> c (h d)"), wv_hi[:, :].bitcast(F32),
                              ALU.subtract).then_inc(split_lo, 1)

            dve.wait_ge(split_hi, 5)
            dve.tensor_tensor(gate_both[:, E1:2 * E1], gate_f[:, 0:E1], gate_hi[:, 0:E1].bitcast(F32), ALU.subtract).then_inc(split_lo, 1)
            dve.wait_ge(split_hi, 6)
            dve.tensor_tensor(w1_lo[0:C + 1, :], w1_f[:, :, :].rearrange("c e h -> c (e h)"), w1_hi[0:C + 1, :].bitcast(F32),
                              ALU.subtract).then_inc(split_lo, 1)
            dve.tensor_copy(b2_lead[:, 0, :], b2_f[:, :]).then_inc(b2_step, 1)
            dve.wait_ge(b2_step, 1)
            dve.tensor_tensor(b2_rest[:, 0, :], b2_f[:, :], b2_lead[:, 0, :], ALU.subtract).then_inc(b2_step, 1)
            dve.wait_ge(b2_step, 2)
            dve.tensor_copy(b2_lead[:, 1, :], b2_rest[:, 0, :]).then_inc(b2_step, 1)
            dve.wait_ge(b2_step, 3)
            dve.tensor_tensor(b2_rest[:, 1, :], b2_rest[:, 0, :], b2_lead[:, 1, :], ALU.subtract).then_inc(b2_step, 1)
            dve.tensor_copy(b2_parts[0:1, :], b2_lead[0:1, 0, :]).then_inc(split_lo, 1)
            dve.tensor_copy(b2_parts[32:33, :], b2_lead[32:33, 1, :]).then_inc(split_lo, 1)
            dve.wait_ge(b2_step, 4)
            dve.tensor_copy(b2_parts[64:65, :], b2_rest[64:65, 1, :]).then_inc(split_lo, 1)

            mix_base = 0
            steps = {}
            stage = FRONT

            def step_done(ins):
                steps[stage] += 1
                ins.then_inc(dve_step[stage], 1)

            def wait_step(n):
                dve.wait_ge(dve_step[stage], at(n, DVE_STEPS[stage], steps[stage]))

            def top_two(n, count, value, beats, before, rank, chosen):
                shape = [P, TILES, count, count]
                of_j = value.unsqueeze(2).to_broadcast(shape)
                of_e = value.unsqueeze(3).to_broadcast(shape)
                greater, equal = beats[:, :, :, 0:count], beats[:, :, :, count:2 * count]
                step_done(dve.tensor_tensor(equal, of_j, of_e, ALU.is_equal))
                step_done(dve.tensor_tensor(greater, of_j, of_e, ALU.is_gt))
                wait_step(n)
                step_done(dve.tensor_tensor(equal, equal, before[:, :, :].unsqueeze(1).to_broadcast(shape), ALU.mult))
                wait_step(n)
                step_done(dve.tensor_reduce(rank[:, :, :], beats[:, :, :, :], AX_X, ALU.add))
                wait_step(n)
                step_done(dve.tensor_scalar(chosen[:, :, :], rank[:, :, :], 1.5, None, ALU.is_lt))
                wait_step(n)

            def row_statistics(n, which, rows):
                base = steps[stage]
                for t in range(TILES):
                    step_done(dve.bn_stats(ln_stats[:, which, t, :], rows[:, t, :]))
                for t in range(TILES):
                    dve.wait_ge(dve_step[stage], at(n, DVE_STEPS[stage], base + t + 1))
                    dve.bn_aggr(ln_mv[:, which, t, :], ln_stats[:, which, t, :]).then_inc(ln_ready[which], UNFUSED)

            def normalise_rows(n, which, rows):
                if not is_first(n):
                    wait_filled(dve, n - 1, (("norm1_t",), ("norm2_t",))[which])
                dve.wait_ge(rstd_ready[which], at(n, 1, 1))
                for t in range(TILES):
                    dve.tensor_scalar(normed[:, which, t, :], rows[:, t, :], ln_mv[:, which, t, 0:1],
                                      ln_scale[:, which, t:t + 1], ALU.subtract, ALU.mult).then_inc(normed_ready[which], 1)

            def body(i, stages, parity):
                nonlocal stage, mix_base
                steps.update({g: 0 for g in STAGES})
                for step, kind, n, odd in steps_of(VECTOR, i, stages, parity):
                    stage = STAGE_OF[kind]
                    first = is_first(n)
                    if kind == "xn":
                        if is_first(n):
                            continue
                        if isinstance(n, int):
                            dve.wait_ge(gn_root, 4)
                        normalise_x(n)
                    elif kind == "norm1":
                        normalise_rows(n, 0, res1s[odd])
                    elif kind == "norm2":
                        normalise_rows(n, 1, res2)
                    elif kind == "ffn2":
                        e = step[1]
                        dve.wait_ge(y_filled, at(n, E1, e + 1 + HIDDEN_FREE))
                        if e == 0:
                            dve.wait_ge(stored[odd], at(n, 8, 8 if odd else 16))
                        for t in range(TILES):
                            dve.wait_ge(y_mixed, at(n, E1 * TILES, TILES * (e - 1) + t + 1 + Y_FREE))
                            dve.scalar_tensor_tensor(
                                results[odd][:, t, :], PS[:, Y_BANK, t * C:(t + 1) * C], weight1[:, t, e:e + 1],
                                res2[:, t, :] if e == 0 else results[odd][:, t, :], ALU.mult, ALU.add).then_inc(y_mixed, 1)
                    elif step == ("gates", 0):
                        wait_act(dve, n, ("conv", TILES - 1))
                        logit = conv_y[:, :, E0 * C:E0 * C + E0]
                        top_two(n, E0, logit, beats0, before0, rank0, chosen0)
                        step_done(dve.tensor_tensor(picked0[:, :, :], chosen0[:, :, :], logit, ALU.mult))
                        wait_step(n)
                        step_done(dve.tensor_reduce(sum0[:, :], picked0[:, :, :], AX_X, ALU.add))
                        wait_step(n)
                        dve.scalar_tensor_tensor(arg0[:, :, :], sum0[:, :].unsqueeze(2).to_broadcast([P, TILES, E0]), -0.5,
                                                 logit, ALU.mult, ALU.add).then_inc(arg0_ready, 1)
                    elif step == ("gates", 1):
                        dve.wait_ge(tanh0_ready, at(n, 1, 1))
                        step_done(dve.tensor_scalar(half0[:, :, :], tanh0[:, :, :], 0.5, 0.5, ALU.mult, ALU.add))
                        wait_step(n)
                        dve.tensor_tensor(weight0[:, :, :], half0[:, :, :], chosen0[:, :, :], ALU.mult).then_inc(weight0_ready, 1)
                        dve.wait_ge(weight0_ready, at(n, 1, 1))
                    elif kind == "mix":
                        e = step[1]
                        if e == 1:
                            mix_base = steps[stage]
                        for t in range(TILES):
                            y = conv_y[:, t, e * C:(e + 1) * C]
                            if e == 1:
                                dve.wait_ge(mix_begun, at(n, TILES, t + 1))
                            else:
                                dve.wait_ge(dve_step[stage], at(n, DVE_STEPS[stage], mix_base + TILES * (e - 2) + t + 1))
                            step_done(dve.scalar_tensor_tensor(mixed[:, t, :], y, weight0[:, t, e:e + 1], mixed[:, t, :],
                                                               ALU.mult, ALU.add))
                    elif kind == "stats1":
                        wait_step(n)
                        step_done(dve.scalar_tensor_tensor(leaky[:, :, :], mixed[:, :, :], 0.01, mixed[:, :, :],
                                                           ALU.mult, ALU.max))
                        wait_step(n)
                        dve.tensor_tensor(res1s[odd][:, :, :], leaky[:, :, :], X[:, bass.ds(n * TILES, TILES), :], ALU.add
                                          ).then_inc(res_ready, 1)
                        dve.wait_ge(res_ready, at(n, 1, 1))
                        row_statistics(n, 0, res1s[odd])
                    elif kind in ("norm1_t", "norm2_t"):
                        lo, hi = (t1_lo, t1_hi) if kind == "norm1_t" else (t2_lo, t2_hi)
                        wait_filled(dve, n, step)
                        wait_act(dve, n, step)
                        dve.tensor_tensor(lo[0:C, :], PS[0:C, bank(step), :], hi[0:C, :].bitcast(F32), ALU.subtract
                                          ).then_inc(dve_drained[stage], 1)
                    elif kind == "qk":
                        tensor = step[1]
                        wait_filled(dve, n, step)
                        wait_act(dve, n, step)
                        if not first:
                            dve.wait_ge(low_ready, at(n - 1, 2 * UNFUSED, (tensor + 1) * UNFUSED))
                        ins = dve.tensor_tensor(qk_rest[:, tensor, :], PS[0:C, bank(step), :],
                                                qk_parts[:, tensor, 0, :], ALU.subtract)
                        ins.then_inc(dve_drained[stage], 1)
                    elif kind == "score":
                        _, b, k = step
                        wait_filled(dve, n, step)
                        ps = PS[:, bank(step), :]
                        if k < 2:
                            width = min(4, HEADS - 4 * k)
                            dst, src = row_max[:, 2 * b, 4 * k:4 * k + width], ps[:, 0:width * P].rearrange("p (h s) -> p h s", s=P)
                        else:
                            dst = row_max[:, 2 * b + 1, 2 * (k - 2):2 * (k - 2) + 2]
                            src = ps.rearrange("p (h s) -> p h s", s=TOKENS)
                        dve.tensor_reduce(dst, src, AX_X, ALU.max).then_inc(dve_drained[stage], 1)
                    elif kind == "shift":
                        wait_dve(dve, n, ("score", 1, 4))
                        if not first:
                            wait_filled(dve, n - 1, step)
                        lead = shift_parts[:, :, 0, :]
                        step_done(dve.tensor_scalar(lead, row_max[:, :, :], -1.0, None, ALU.mult))
                        wait_step(n)
                        step_done(dve.scalar_tensor_tensor(shift_rest[:, :, :], row_max[:, :, :], -1.0, lead,
                                                           ALU.mult, ALU.subtract))
                        wait_step(n)
                        step_done(dve.tensor_copy(shift_parts[:, :, 1, :], shift_rest[:, :, :]))
                        wait_step(n)
                        dve.tensor_tensor(shift_parts[:, :, 2, :], shift_rest[:, :, :], shift_parts[:, :, 1, :], ALU.subtract
                                          ).then_inc(shift_ready, 1)
                    elif kind == "out_t":
                        b = step[1]
                        wait_filled(dve, n, step)
                        rows = PS[:, bank(step), 0:4 * C].rearrange("p (n d) -> p n d", d=HS)
                        step_done(dve.reciprocal(inv_sum[:, b, :], rows[:, :, D]))
                        wait_step(n)
                        if b == 0 and not first:
                            wait_filled(dve, n - 1, ("heads_t",))
                        dve.tensor_tensor(att[:, 2 * b:2 * b + 2, :].rearrange("p t (h d) -> p (t h) d", d=D),
                                          rows[:, :, 0:D], inv_sum[:, b, :].unsqueeze(2).to_broadcast([P, 4 * HG, D]),
                                          ALU.mult).then_inc(dve_drained[stage], 1)
                    elif kind == "proj":
                        wait_filled(dve, n, step)
                        if not first:
                            dve.wait_ge(y_mixed, at(n - 1, E1 * TILES, TILES + Y_FREE))
                        dve.tensor_tensor(res2[:, :, :].rearrange("p t c -> p (t c)"), PS[:, bank(step), 0:TILES * C],
                                          res1s[odd][:, :, :].rearrange("p t c -> p (t c)"), ALU.add).then_inc(dve_drained[stage], 1)
                        wait_dve(dve, n, step)
                        row_statistics(n, 1, res2)
                    elif kind == "gate2":
                        wait_filled(dve, n, step)
                        ps = PS[:, bank(step), 0:TILES * C].rearrange("p (t c) -> p t c", c=C)
                        step_done(dve.tensor_copy(gcross[:, :, :], ps[:, :, E1:2 * E1]))
                        wait_step(n)
                        dve.tensor_tensor(glogit[:, :, :], ps[:, :, 0:E1], gcross[:, :, :], ALU.add
                                          ).then_inc(dve_drained[stage], 1)
                        wait_dve(dve, n, step)
                        step_done(dve.tensor_reduce(gmax[:, :], glogit[:, :, :], AX_X, ALU.max))
                        wait_step(n)
                        wide = [P, TILES, E1]
                        dve.tensor_tensor(gdiff[:, :, :], glogit[:, :, :], gmax[:, :].unsqueeze(2).to_broadcast(wide),
                                          ALU.subtract).then_inc(gdiff_ready, 1)
                        top_two(n, E1, glogit[:, :, :], beats1, before1, rank1, chosen1)
                    elif kind == "weights":
                        wide = [P, TILES, E1]
                        dve.wait_ge(gexp_ready, at(n, 1, 1))
                        step_done(dve.tensor_tensor(gpick[:, :, :], gexp[:, :, :], chosen1[:, :, :], ALU.mult))
                        step_done(dve.tensor_reduce(gsum[:, :], gexp[:, :, :], AX_X, ALU.add))
                        wait_step(n)
                        step_done(dve.tensor_reduce(gpsum[:, :], gpick[:, :, :], AX_X, ALU.add))
                        wait_step(n)
                        step_done(dve.scalar_tensor_tensor(gpeps[:, :], gsum[:, :], 1e-9, gpsum[:, :], ALU.mult, ALU.add))
                        wait_step(n)
                        step_done(dve.reciprocal(gpinv[:, :], gpeps[:, :]))
                        wait_step(n)
                        dve.wait_ge(y_mixed, at(n, E1 * TILES, Y_FREE))
                        step_done(dve.tensor_tensor(weight1[:, :, :], gpick[:, :, :], gpinv[:, :].unsqueeze(2).to_broadcast(wide),
                                                    ALU.mult))
                        wait_step(n)
                assert all(steps[g] == DVE_STEPS[g] for g in stages), steps

            iterations(dve, body)


_INS = ["x", "L0_conv_Wg", "L0_conv_We", "L0_conv_be", "L1_attn_wk", "L1_attn_wq", "L1_attn_wv", "L1_attn_wproj",
        "L1_attn_bproj", "L1_ffn_gate_w", "L1_ffn_gate_b", "L1_ffn_w1", "L1_ffn_b1", "L1_ffn_w2", "L1_ffn_b2"]
_OUTS = [((IMAGES, 16, 16, C), "float32")]


def kernel(**inputs):
    import numpy as _np
    import concourse.bacc as _bacc
    from concourse import mybir as _mybir
    from concourse.bass_utils import run_bass_kernel_spmd as _run

    nc = _bacc.Bacc("TRN2", target_bir_lowering=False, num_devices=1)
    arrays, args = {}, []
    for name in _INS:
        a = _np.ascontiguousarray(inputs[name])
        arrays[f"in_{name}_dram"] = a
        args.append(nc.dram_tensor(f"in_{name}_dram", a.shape, _mybir.dt.from_np(a.dtype), kind="ExternalInput").ap())
    for i, (shape, dtype) in enumerate(_OUTS):
        dt = _mybir.dt.from_np(_np.dtype(dtype))
        args.append(nc.dram_tensor(f"out_{i}_dram", shape, dt, kind="ExternalOutput").ap())
    build(nc, *args)
    r = _run(nc, [arrays], core_ids=[0])
    got = tuple(r.results[0][f"out_{i}_dram"] for i in range(len(_OUTS)))
    return got[0]
```
